# Optimizing a Trainium2 kernel written in Bass

```python
import numpy as np
import jax
import jax.numpy as jnp

def _softmax(x, axis=-1):
    return jax.nn.softmax(x, axis=axis)

def _gelu(x):
    return jax.nn.gelu(x, approximate=True)

def _silu(x):
    return jax.nn.silu(x)

def _sigmoid(x):
    return jax.nn.sigmoid(x)

def _layernorm(x, axis=-1, eps=1e-05):
    m = jnp.mean(x, axis=axis, keepdims=True)
    v = jnp.var(x, axis=axis, keepdims=True)
    return (x - m) / jnp.sqrt(v + eps)

def _scatter_add(tgt, idx, src, axis=0):
    return tgt.at[idx].add(src)

def _segment_sum(src, seg, n):
    return jax.ops.segment_sum(src, seg, n)
kernel_name = 'mk_gnn_resnorm_d2_gnn_r32_1da2dc'

def setup_inputs(seed: int=0):
    np.random.seed(seed)
    _w = jnp.asarray

    def _rec_inputs():
        import jax
        import jax.numpy as jnp
        _gk = jax.random.key(seed)
        x = -0.000202 + 1 * jax.random.normal(jax.random.fold_in(_gk, 1), (50000, 128), jnp.float32)
        src = jax.random.randint(jax.random.fold_in(_gk, 2), (25000,), 0, 50000, jnp.int32)
        dst = jnp.minimum((50000 * jax.random.uniform(jax.random.fold_in(_gk, 3), (25000,)) ** 2.0).astype(jnp.int32), 49999)
        _o = jnp.argsort(dst, stable=True)
        src = src[_o]
        dst = dst[_o]
        edge_type_9 = jax.random.randint(jax.random.fold_in(_gk, 12), (25000,), 0, 9, jnp.int32)
        edge_weight = jax.random.uniform(jax.random.fold_in(_gk, 13), (25000,), jnp.float32, 0.0, 0.999998)
        return (x, src, dst, edge_type_9, edge_weight)
    x, src, dst, edge_type_9, edge_weight = _rec_inputs()

    def _L0_gnn_setup():
        import jax, jax.numpy as jnp
        import numpy as np
        N, C, E = (50000, 128, 18750)
        EPS = 1e-05
        SLOPE = 0.2

        def layer_norm(h, g, b):
            m = jnp.mean(h, axis=-1, keepdims=True)
            v = jnp.mean((h - m) ** 2, axis=-1, keepdims=True)
            return (h - m) * jax.lax.rsqrt(v + EPS) * g + b
        key = jax.random.key(seed)
        ks = jax.random.split(key, 12)
        s1 = 1.0 / np.sqrt(2 * C)
        s2 = 1.0 / np.sqrt(C)
        return {'x': jax.random.normal(ks[0], (N, C), dtype=jnp.float32), 'edge_index': jax.random.randint(ks[1], (2, E), 0, N, dtype=jnp.int64), 'edge_attr': jax.random.uniform(ks[2], (E,), dtype=jnp.float32), 'w1': jax.random.uniform(ks[3], (2 * C, C), jnp.float32, -s1, s1), 'b1': jax.random.uniform(ks[4], (C,), jnp.float32, -s1, s1), 'g1': jnp.ones((C,), jnp.float32), 'be1': jnp.zeros((C,), jnp.float32), 'w2': jax.random.uniform(ks[5], (C, C), jnp.float32, -s2, s2), 'b2': jax.random.uniform(ks[6], (C,), jnp.float32, -s2, s2), 'g2': jnp.ones((C,), jnp.float32), 'be2': jnp.zeros((C,), jnp.float32)}
    _L0_gnn_all = _L0_gnn_setup()
    _L0_gnn_in = {k: v for k, v in _L0_gnn_all.items() if k in ('w1', 'b1', 'g1', 'be1', 'w2', 'b2', 'g2', 'be2')}
    del _L0_gnn_all

    def _L1_gnn_setup():
        import jax, jax.numpy as jnp
        import numpy as np
        NUM_EDGE_TYPES = 8
        HIDDEN = 128
        N_NODES = 50000
        N_EDGES = 18750

        def _gru_cell(x, h, W_ih, W_hh, b_ih, b_hh):
            H = h.shape[-1]
            gi = x @ W_ih.T + b_ih
            gh = h @ W_hh.T + b_hh
            i_r, i_z, i_n = (gi[:, :H], gi[:, H:2 * H], gi[:, 2 * H:])
            h_r, h_z, h_n = (gh[:, :H], gh[:, H:2 * H], gh[:, 2 * H:])
            r = jax.nn.sigmoid(i_r + h_r)
            z = jax.nn.sigmoid(i_z + h_z)
            n = jnp.tanh(i_n + r * h_n)
            return (1.0 - z) * n + z * h
        key = jax.random.key(seed)
        ks = jax.random.split(key, 10)
        H = HIDDEN
        h = jax.random.normal(ks[0], (N_NODES, H), dtype=jnp.float32)
        edge_index = jax.random.randint(ks[1], (2, N_EDGES), 0, N_NODES, dtype=jnp.int32)
        edge_type = jax.random.randint(ks[2], (N_EDGES,), 0, NUM_EDGE_TYPES + 1, dtype=jnp.int32)
        s = 1.0 / np.sqrt(H)
        W_msg = jax.random.uniform(ks[3], (H, H), jnp.float32, -s, s)
        b_msg = jax.random.uniform(ks[4], (H,), jnp.float32, -s, s)
        edge_embed = jax.random.normal(ks[5], (NUM_EDGE_TYPES + 1, H), dtype=jnp.float32)
        W_ih = jax.random.uniform(ks[6], (3 * H, H), jnp.float32, -s, s)
        W_hh = jax.random.uniform(ks[7], (3 * H, H), jnp.float32, -s, s)
        b_ih = jax.random.uniform(ks[8], (3 * H,), jnp.float32, -s, s)
        b_hh = jax.random.uniform(ks[9], (3 * H,), jnp.float32, -s, s)
        return {'h': h, 'edge_index': edge_index, 'edge_type': edge_type, 'num_nodes': N_NODES, 'W_msg': W_msg, 'b_msg': b_msg, 'edge_embed': edge_embed, 'W_ih': W_ih, 'W_hh': W_hh, 'b_ih': b_ih, 'b_hh': b_hh}
    _L1_gnn_all = _L1_gnn_setup()
    _L1_gnn_in = {k: v for k, v in _L1_gnn_all.items() if k in ('W_msg', 'b_msg', 'edge_embed', 'W_ih', 'W_hh', 'b_ih', 'b_hh')}
    del _L1_gnn_all
    return {'x': x, 'src': src, 'dst': dst, 'edge_type_9': edge_type_9, 'edge_weight': edge_weight, 'L0_gnn_w1': _L0_gnn_in['w1'], 'L0_gnn_b1': _L0_gnn_in['b1'], 'L0_gnn_g1': _L0_gnn_in['g1'], 'L0_gnn_be1': _L0_gnn_in['be1'], 'L0_gnn_w2': _L0_gnn_in['w2'], 'L0_gnn_b2': _L0_gnn_in['b2'], 'L0_gnn_g2': _L0_gnn_in['g2'], 'L0_gnn_be2': _L0_gnn_in['be2'], 'L1_gnn_W_msg': _L1_gnn_in['W_msg'], 'L1_gnn_b_msg': _L1_gnn_in['b_msg'], 'L1_gnn_edge_embed': _L1_gnn_in['edge_embed'], 'L1_gnn_W_ih': _L1_gnn_in['W_ih'], 'L1_gnn_W_hh': _L1_gnn_in['W_hh'], 'L1_gnn_b_ih': _L1_gnn_in['b_ih'], 'L1_gnn_b_hh': _L1_gnn_in['b_hh']}

def reference(x, src, dst, edge_type_9, edge_weight, L0_gnn_w1, L0_gnn_b1, L0_gnn_g1, L0_gnn_be1, L0_gnn_w2, L0_gnn_b2, L0_gnn_g2, L0_gnn_be2, L1_gnn_W_msg, L1_gnn_b_msg, L1_gnn_edge_embed, L1_gnn_W_ih, L1_gnn_W_hh, L1_gnn_b_ih, L1_gnn_b_hh):
    import jax
    import jax.numpy as jnp

    def _L0_gnn_ref(x, edge_index, edge_attr, w1, b1, g1, be1, w2, b2, g2, be2):
        import jax, jax.numpy as jnp
        import numpy as np
        N, C, E = (50000, 128, 18750)
        EPS = 1e-05
        SLOPE = 0.2

        def layer_norm(h, g, b):
            m = jnp.mean(h, axis=-1, keepdims=True)
            v = jnp.mean((h - m) ** 2, axis=-1, keepdims=True)
            return (h - m) * jax.lax.rsqrt(v + EPS) * g + b
        source, target = (edge_index[0], edge_index[1])
        ef = jnp.concatenate([x[source], x[target]], axis=1)
        h = jax.nn.leaky_relu(layer_norm(ef @ w1 + b1, g1, be1), SLOPE)
        h = jax.nn.leaky_relu(layer_norm(h @ w2 + b2, g2, be2), SLOPE)
        h = h * edge_attr[:, None]
        out = jax.ops.segment_sum(h, target, num_segments=N)
        return out

    def _L1_gnn_ref(h, edge_index, edge_type, num_nodes, W_msg, b_msg, edge_embed, W_ih, W_hh, b_ih, b_hh):
        import jax, jax.numpy as jnp
        import numpy as np
        NUM_EDGE_TYPES = 8
        HIDDEN = 128
        N_NODES = 50000
        N_EDGES = 18750

        def _gru_cell(x, h, W_ih, W_hh, b_ih, b_hh):
            H = h.shape[-1]
            gi = x @ W_ih.T + b_ih
            gh = h @ W_hh.T + b_hh
            i_r, i_z, i_n = (gi[:, :H], gi[:, H:2 * H], gi[:, 2 * H:])
            h_r, h_z, h_n = (gh[:, :H], gh[:, H:2 * H], gh[:, 2 * H:])
            r = jax.nn.sigmoid(i_r + h_r)
            z = jax.nn.sigmoid(i_z + h_z)
            n = jnp.tanh(i_n + r * h_n)
            return (1.0 - z) * n + z * h
        src = edge_index[0]
        dst = edge_index[1]
        src_h = h[src] @ W_msg.T + b_msg
        emb = edge_embed[jnp.clip(edge_type, 0, NUM_EDGE_TYPES)]
        msg = src_h + emb
        messages = jax.ops.segment_sum(msg, dst, num_segments=num_nodes)
        h_new = _gru_cell(messages, h[:num_nodes], W_ih, W_hh, b_ih, b_hh)
        result = jnp.zeros_like(h).at[:num_nodes].set(h_new)
        return result
    edge_index = jnp.stack([src, dst])
    x = _layernorm(x + _L0_gnn_ref(x, edge_index, edge_weight, L0_gnn_w1, L0_gnn_b1, L0_gnn_g1, L0_gnn_be1, L0_gnn_w2, L0_gnn_b2, L0_gnn_g2, L0_gnn_be2), axis=-1)
    x = _layernorm(x + _L1_gnn_ref(x, edge_index, edge_type_9, 50000, L1_gnn_W_msg, L1_gnn_b_msg, L1_gnn_edge_embed, L1_gnn_W_ih, L1_gnn_W_hh, L1_gnn_b_ih, L1_gnn_b_hh), axis=-1)
    return x

_drawn_inputs = setup_inputs


def setup_inputs(seed=0):
    import zlib

    import numpy as np

    out = dict(_drawn_inputs(seed))
    spreads = {'L0_gnn_g1': (1.0, 0.2),
     'L0_gnn_be1': (0.0, 0.321),
     'L0_gnn_g2': (1.0, 0.2),
     'L0_gnn_be2': (0.0, 0.273)}
    factors = {'L0_gnn_b1': 3.191, 'L1_gnn_b_msg': 6.959, 'L1_gnn_b_ih': 3.18, 'L1_gnn_b_hh': 4.939}
    for name, (base, spread) in spreads.items():
        noise = np.random.default_rng([zlib.crc32(name.encode()), seed]).standard_normal(out[name].shape)
        drawn = base * np.exp(spread * noise) if base else spread * noise
        out[name] = jnp.asarray(drawn.astype(out[name].dtype))
    for name, factor in factors.items():
        out[name] = (out[name] * factor).astype(out[name].dtype)
    return out
```

```python
from contextlib import ExitStack

import concourse.bass as bass
from concourse import mybir

F32 = mybir.dt.float32
I32 = mybir.dt.int32
ALU = mybir.AluOpType
ACT = mybir.ActivationFunctionType

P = 128
K = 4
W = K * P
RING = 4
EPS = 1e-5
SLOPE = 0.2
DMA = 16


def gnn_kernel(nc, x, src, dst, edge_type, edge_weight, w1, b1, g1, be1, w2, b2, g2, be2,
               W_msg, b_msg, edge_embed, W_ih, W_hh, b_ih, b_hh, out):
    N, H = x.shape
    E = src.shape[0]
    T_TYPES = edge_embed.shape[0]
    NB = -(-E // W)
    TILES = NB * K
    HALF = TILES // 2
    FULL_G = N // W
    NG = FULL_G + 1
    ROWS = -(-(N + W) // (16 * P)) * 16 * P
    ZCOLS = 2048
    ZCHUNKS = ROWS * H // (P * ZCOLS)
    assert H == P and TILES == 2 * HALF and HALF <= P and ZCHUNKS * ZCOLS * P == ROWS * H
    whole_rows = E // P - HALF
    rest = E - (E // P) * P
    assert rest and whole_rows == HALF - 1
    PAD_TARGET = N + (K - 1) * P

    def eq_at(k):
        return P * k * (k + 1) // 2

    agg = nc.dram_tensor("agg", [ROWS, H], F32, kind="Internal").ap()
    msum = nc.dram_tensor("msum", [ROWS, H], F32, kind="Internal").ap()
    x1 = nc.dram_tensor("x1", [N, H], F32, kind="Internal").ap()
    dpad = nc.dram_tensor("dpad", [NB, W], I32, kind="Internal").ap()

    def groups(t):
        return (t[0:FULL_G * W, :].rearrange("(g p j) f -> g p (j f)", p=P, j=K),
                t[N - W:N, :].rearrange("(p j) f -> p (j f)", p=P))

    def group(t, g):
        whole, last = groups(t)
        return last if isinstance(g, int) and g == NG - 1 else whole[g]

    ctx = ExitStack()
    with ctx:
        def sb(name, shape, dt=F32):
            return ctx.enter_context(nc.sbuf_tensor(name, shape, dt))

        def sem(name):
            return ctx.enter_context(nc.semaphore(name))

        def sem_ring(name):
            return [sem(f"{name}{s}") for s in range(RING)]

        bank = [ctx.enter_context(nc.psum_tensor(f"bank{b}", [P, W], F32)) for b in range(6)]
        turned_ps = ctx.enter_context(nc.psum_tensor("turned_ps", [P, 2 * W], F32))

        ident = sb("ident", [P, P])
        ones_row = sb("ones_row", [1, P])
        before = sb("before", [P, W])
        zeros = sb("zeros", [P, ZCOLS])
        eps_col = sb("eps_col", [P, 1])
        w1_sb = sb("w1_sb", [P, 2, P])
        w2_sb = sb("w2_sb", [P, P])
        b1_row = sb("b1_row", [1, P])
        b2_row = sb("b2_row", [1, P])
        g1_col = sb("g1_col", [P, 1])
        be1_col = sb("be1_col", [P, 1])
        g2_all = sb("g2_all", [P, P])
        be2_all = sb("be2_all", [P, P])
        wmsg_raw = sb("wmsg_raw", [P, P])
        wih_raw = sb("wih_raw", [P, 3, P])
        whh_raw = sb("whh_raw", [P, 3, P])
        wmsg_t = sb("wmsg_t", [P, P])
        wih_t = sb("wih_t", [P, 3 * P])
        whh_t = sb("whh_t", [P, 3 * P])
        bih_col = sb("bih_col", [P, 3])
        bhh_col = sb("bhh_col", [P, 3])
        brz_col = sb("brz_col", [P, 2])
        emb_sb = sb("emb_sb", [T_TYPES, P])
        bmsg_all = sb("bmsg_all", [T_TYPES, P])
        embb = sb("embb", [T_TYPES, P])
        type_no = sb("type_no", [P, T_TYPES])
        rows_i = sb("rows_i", [P, 3, 2, P], I32)
        rows_f = sb("rows_f", [P, 4, 2, P])
        gather_idx = sb("gather_idx", [P, NB, 2 * K], I32)
        scatter_idx = sb("scatter_idx", [P, NB, K], I32)
        dst_col = sb("dst_col", [P, NB, K])
        spill_row = sb("spill_row", [P, NB, K], I32)
        to_spill = sb("to_spill", [P, NB, K])
        type_col = sb("type_col", [P, NB, K])
        w_col = sb("w_col", [P, NB, K])
        gidx_slot = sb("gidx_slot", [P, RING, 2 * K], I32)
        sidx_slot = sb("sidx_slot", [P, RING, K], I32)
        xg = sb("xg", [P, RING, 2 * K, P])
        dst_row = sb("dst_row", [P, 2, W], I32)
        equal = sb("equal", [P, 2, eq_at(K)])
        junk = sb("junk", [P, K, W])
        dups = sb("dups", [P, 2, K])
        moved = sb("moved", [P, 2, K])
        xt = sb("xt", [P, 2, 2 * W])
        h1n = sb("h1n", [P, 2, W])
        y1 = sb("y1", [P, 2, W])
        act1 = sb("act1", [P, 2, W])
        h2n = sb("h2n", [P, W])
        h2g = sb("h2g", [P, W])
        h2b = sb("h2b", [P, W])
        hout = sb("hout", [P, 2, W])
        total = sb("total", [P, RING, W])
        stats = sb("stats", [P, 2, K, 6])
        mv = sb("mv", [P, 2, K, 2])
        std = sb("std", [P, 2, K])
        rstd = sb("rstd", [P, 2, K])
        onehot = sb("onehot", [P, 2, K, T_TYPES])
        at_sb = sb("at_sb", [P, 2, W])
        ct_sb = sb("ct_sb", [T_TYPES, 2, W])
        ng_x = sb("ng_x", [P, RING, W])
        ng_s = sb("ng_s", [P, RING, W])
        n_stats = sb("n_stats", [P, 2, K, 6])
        n_mv = sb("n_mv", [P, 2, K, 2])
        n_var = sb("n_var", [P, 2, K])
        minus_half = sb("minus_half", [P, K])
        n_rstd = sb("n_rstd", [P, 2, K])
        mt = sb("mt", [P, 2, W])
        xt1 = sb("xt1", [P, RING, W])
        r_sb = sb("r_sb", [P, 2, W])
        z_sb = sb("z_sb", [P, 2, W])
        rh_sb = sb("rh_sb", [P, 2, W])
        pre_n = sb("pre_n", [P, 2, W])
        n_sb = sb("n_sb", [P, 2, W])
        hm_sb = sb("hm_sb", [P, 2, W])
        zh_sb = sb("zh_sb", [P, 2, W])
        hf_sb = sb("hf_sb", [P, 2, W])
        y_sb = sb("y_sb", [P, 2, W])
        o_sb = ng_s

        pool_set = sem("pool_set")
        pads_set = sem("pads_set")
        edges_in = sem("edges_in")
        weights_in = sem("weights_in")
        rows_ready = sem("rows_ready")
        setup_turned = sem("setup_turned")
        weights_ready = sem("weights_ready")
        cols_made = sem("cols_made")
        index_ready = sem("index_ready")
        dpad_out = sem("dpad_out")
        zeroed = sem("zeroed")
        passed = sem("passed")
        gidx_copied = sem("gidx_copied")
        sidx_copied = sem("sidx_copied")
        gathered = sem_ring("gathered")
        dstrow_in = [sem("dstrow_in0"), sem("dstrow_in1")]
        equal_made = sem("equal_made")
        dup_done = sem("dup_done")
        moved_done = sem("moved_done")
        sidx_made = sem("sidx_made")
        xg_turned = sem("xg_turned")
        xt_ready = sem("xt_ready")
        h1_done = sem("h1_done")
        st1_done = sem("st1_done")
        mv1_ready = sem("mv1_ready")
        std1_ready = sem("std1_ready")
        rstd1_ready = sem("rstd1_ready")
        h1n_ready = sem("h1n_ready")
        h1n_turned = sem("h1n_turned")
        y1_ready = sem("y1_ready")
        act1_ready = sem("act1_ready")
        h2_done = sem("h2_done")
        st2_done = sem("st2_done")
        mv2_ready = sem("mv2_ready")
        std2_ready = sem("std2_ready")
        rstd2_ready = sem("rstd2_ready")
        h2n_ready = sem("h2n_ready")
        h2g_ready = sem("h2g_ready")
        h2b_ready = sem("h2b_ready")
        hout_ready = sem("hout_ready")
        sums_done = sem("sums_done")
        total_ready = sem("total_ready")
        scattered = sem("scattered")
        x_in = sem_ring("x_in")
        agg_in = sem_ring("agg_in")
        res_ready = sem("res_ready")
        nst_done = sem("nst_done")
        nmv_ready = sem("nmv_ready")
        neps_done = sem("neps_done")
        nrstd_ready = sem("nrstd_ready")
        x1_ready = sem("x1_ready")
        x1_out = sem_ring("x1_out")
        gidx1_copied = sem("gidx1_copied")
        sidx1_copied = sem("sidx1_copied")
        gathered1 = sem_ring("gathered1")
        dstrow1_in = [sem("dstrow1_in0"), sem("dstrow1_in1")]
        equal1_made = sem("equal1_made")
        edge_sums = sem("edge_sums")
        at_ready = sem("at_ready")
        msg_done = sem("msg_done")
        msg_ready = sem("msg_ready")
        scattered1 = sem("scattered1")
        s_in = sem_ring("s_in")
        x1_in = sem_ring("x1_in")
        g_turned = sem("g_turned")
        mt_ready = sem("mt_ready")
        xt1_ready = sem("xt1_ready")
        r_done = sem("r_done")
        hn_done = sem("hn_done")
        z_done = sem("z_done")
        in_done = sem("in_done")
        r_ready = sem("r_ready")
        z_ready = sem("z_ready")
        rh_ready = sem("rh_ready")
        pre_ready = sem("pre_ready")
        n_ready = sem("n_ready")
        hm_ready = sem("hm_ready")
        zh_ready = sem("zh_ready")
        hf_ready = sem("hf_ready")
        back_done = sem("back_done")
        y_ready = sem("y_ready")
        yst_done = sem("yst_done")
        ymv_ready = sem("ymv_ready")
        yeps_done = sem("yeps_done")
        yrstd_ready = sem("yrstd_ready")
        o_ready = sem("o_ready")
        out_done = sem_ring("out_done")

        def steps(eng, count, step, lag=0):
            for i in range(RING):
                step(i, i, 0)
            turns = count // RING
            with eng.Fori(1, turns) as j:
                for s in range(RING):
                    step(j * RING + s, s, j)
            for i in range(turns * RING, count + lag):
                step(i, i % RING, i // RING)

        def in_range(i, n):
            return not isinstance(i, int) or 0 <= i < n

        def wait(eng, s, value):
            if not isinstance(value, int) or value > 0:
                eng.wait_ge(s, value)

        def hold(eng, s, value):
            if not isinstance(value, int):
                eng.wait_ge(s, value)
                eng.sem_inc(passed, 1)
            elif value > 0:
                eng.wait_ge(s, value)
                eng.sem_inc(passed, 1)

        block = ctx.enter_context(nc.Block())

        @block.sync
        def _(sp):
            hold(sp, pads_set, 4)
            edge_loads = 0
            whole = HALF * P
            for n, a in enumerate((src, dst, edge_type, edge_weight)):
                to = rows_i[:, n] if n < 3 else rows_f[:, 3]
                sp.dma_start(to[0:HALF, 0, :], a[0:whole].rearrange("(q e) -> q e", e=P)).then_inc(edges_in, DMA)
                sp.dma_start(to[0:whole_rows, 1, :],
                             a[whole:whole + whole_rows * P].rearrange("(q e) -> q e", e=P)).then_inc(edges_in, DMA)
                sp.dma_start(to[whole_rows:HALF, 1, 0:rest],
                             a[E - rest:E].rearrange("(q e) -> q e", q=1)).then_inc(edges_in, DMA)
                edge_loads += 3
            with nc.allow_non_contiguous_dma(reason="columns of a few hundred bytes"):
                loads = [
                    (w1_sb[:, :, :], w1.rearrange("(h k) n -> k h n", h=2)), (w2_sb[:, :], w2),
                    (b1_row[:, :], b1.rearrange("(a n) -> a n", a=1)), (b2_row[:, :], b2.rearrange("(a n) -> a n", a=1)),
                    (g1_col[:, :], g1.rearrange("(n a) -> n a", a=1)), (be1_col[:, :], be1.rearrange("(n a) -> n a", a=1)),
                    (g2_all[:, :], g2.partition_broadcast(P)), (be2_all[:, :], be2.partition_broadcast(P)),
                    (wmsg_raw[:, :], W_msg), (wih_raw[:, :, :], W_ih.rearrange("(b p) k -> p b k", b=3)),
                    (whh_raw[:, :, :], W_hh.rearrange("(b p) k -> p b k", b=3)),
                    (bih_col[:, :], b_ih.rearrange("(b p) -> p b", b=3)), (bhh_col[:, :], b_hh.rearrange("(b p) -> p b", b=3)),
                    (emb_sb[:, :], edge_embed), (bmsg_all[:, :], b_msg.partition_broadcast(T_TYPES)),
                ]
                assert len(loads) == WEIGHT_LOADS and edge_loads == EDGE_LOADS
                for to, a in loads:
                    sp.dma_start(to, a).then_inc(weights_in, DMA)
            hold(sp, edges_in, EDGE_LOADS * DMA)
            sp.dma_start(dpad.rearrange("b w -> (b w)").rearrange("(c q e) -> q c e", c=2, e=P),
                         rows_i[0:HALF, 1]).then_inc(dpad_out, DMA)
            hold(sp, cols_made, 1)
            for t in (agg, msum):
                tv = t.rearrange("(p r) f -> p (r f)", p=P)
                for z in range(ZCHUNKS):
                    sp.dma_start(tv[:, z * ZCOLS:(z + 1) * ZCOLS], zeros[:, :]).then_inc(zeroed, DMA)

            hold(sp, dpad_out, DMA)

            def load_targets(i, s, _):
                hold(sp, sidx_made, i - 1)
                sp.dma_start(dst_row[:, s % 2, :], dpad[i].partition_broadcast(P))\
                    .then_inc(dstrow_in[s % 2], DMA)
            steps(sp, NB, load_targets)

            hold(sp, scattered, NB * K * DMA)

            def load_nodes(g, s, j):
                hold(sp, x1_out[s], j * DMA)
                sp.dma_start(ng_x[:, s, :], group(x, g)).then_inc(x_in[s], DMA)
                sp.dma_start(ng_s[:, s, :], group(agg, g)).then_inc(agg_in[s], DMA)
            steps(sp, NG, load_nodes)

            def load_targets1(i, s, _):
                hold(sp, equal1_made, i - 1)
                sp.dma_start(dst_row[:, s % 2, :], dpad[i].partition_broadcast(P))\
                    .then_inc(dstrow1_in[s % 2], DMA)
            steps(sp, NB, load_targets1)

            hold(sp, scattered1, NB * K * DMA)

            def load_nodes1(g, s, j):
                hold(sp, out_done[s], j * DMA)
                sp.dma_start(ng_s[:, s, :], group(msum, g)).then_inc(s_in[s], DMA)
                sp.dma_start(ng_x[:, s, :], group(x1, g)).then_inc(x1_in[s], DMA)
            steps(sp, NG, load_nodes1)

        @block.gpsimd
        def _(pool):
            nc.gpsimd.memset(rows_i[:, 0], 0).then_inc(pads_set, 1)
            nc.gpsimd.iota(rows_i[:, 1], [[0, 2], [1, P]], base=PAD_TARGET, channel_multiplier=0).then_inc(pads_set, 1)
            nc.gpsimd.memset(rows_i[:, 2], 0).then_inc(pads_set, 1)
            nc.gpsimd.memset(rows_f[:, 3], 0.0).then_inc(pads_set, 1)
            nc.gpsimd.memset(ident[:, :], 0.0).then_inc(pool_set, 1)
            nc.gpsimd.memset(before[:, :], 1.0).then_inc(pool_set, 1)
            pool.wait_ge(pool_set, 2)
            nc.gpsimd.affine_select(out=ident[:, :], in_=ident[:, :], compare_op=ALU.not_equal, fill=1.0, base=0,
                                    pattern=[[-1, P]], channel_multiplier=1).then_inc(pool_set, 1)
            nc.gpsimd.affine_select(out=before[:, W - P:], in_=before[:, W - P:], compare_op=ALU.is_gt, fill=0.0,
                                    base=0, pattern=[[-1, P]], channel_multiplier=1).then_inc(pool_set, 1)
            nc.gpsimd.iota(spill_row[:, :, :], [[0, NB], [P, K]], base=N, channel_multiplier=1).then_inc(pool_set, 1)
            nc.gpsimd.memset(minus_half[:, :], -0.5).then_inc(pool_set, 1)
            nc.gpsimd.iota(type_no[:, :], [[1, T_TYPES]], base=0, channel_multiplier=0,
                           allow_small_or_imprecise_dtypes=True).then_inc(pool_set, 1)

            def scatter(i, s, table, values_ready, copied, done, indices_ready):
                wait_indices = indices_ready
                if wait_indices is not None:
                    hold(pool, wait_indices, i + 1)
                nc.gpsimd.tensor_copy(sidx_slot[:, s, :], scatter_idx[:, i, :]).then_inc(copied, 1)
                hold(pool, copied, i + 1)
                hold(pool, values_ready, i + 1)
                hold(pool, done, i * K * DMA)
                for k in range(K):
                    nc.gpsimd.indirect_dma_start(
                        table, bass.IndirectOffsetOnAxis(ap=sidx_slot[:, s, k:k + 1], axis=0),
                        total[:, s, k * P:(k + 1) * P], None, compute_op=ALU.add).then_inc(done, DMA)

            def gather(i, s, table, width, slot_free, copied, done):
                hold(pool, slot_free, i - RING + 1)
                nc.gpsimd.tensor_copy(gidx_slot[:, s, 0:width], gather_idx[:, i, 0:width]).then_inc(copied, 1)
                hold(pool, copied, i + 1)
                for k in range(width):
                    nc.gpsimd.indirect_dma_start(
                        xg[:, s, k, :], None, table,
                        bass.IndirectOffsetOnAxis(ap=gidx_slot[:, s, k:k + 1], axis=0)).then_inc(done[s], DMA)

            hold(pool, index_ready, 1)
            for i in range(RING):
                gather(i, i, x, 2 * K, xg_turned, gidx_copied, gathered)
            hold(pool, zeroed, 2 * ZCHUNKS * DMA)

            def edge_step(i, s, _):
                scatter(i, s, agg, total_ready, sidx_copied, scattered, sidx_made)
                if in_range(i + RING, NB):
                    gather(i + RING, s, x, 2 * K, xg_turned, gidx_copied, gathered)
            for i in range(RING):
                edge_step(i, i, 0)
            turns = (NB - RING) // RING
            with pool.Fori(1, turns) as j:
                for s in range(RING):
                    edge_step(j * RING + s, s, j)
            for i in range(turns * RING, NB):
                edge_step(i, i % RING, turns)

            def inverse_std(c, added, value, ready):
                nc.gpsimd.tensor_scalar(n_var[:, c, :], n_mv[:, c, :, 1], EPS, None, ALU.add).then_inc(added, 1)
                hold(pool, added, value)
                nc.gpsimd.tensor_tensor(n_rstd[:, c, :], n_var[:, c, :], minus_half[:, :], ALU.pow).then_inc(ready, 1)

            def node_step(g, s, j):
                if in_range(g, NG):
                    hold(pool, x_in[s], (j + 1) * DMA)
                    hold(pool, agg_in[s], (j + 1) * DMA)
                    nc.gpsimd.tensor_tensor(ng_s[:, s, :], ng_s[:, s, :], ng_x[:, s, :], ALU.add)\
                        .then_inc(res_ready, 1)
                if in_range(g - 1, NG):
                    hold(pool, nmv_ready, g)
                    inverse_std((s - 1) % 2, neps_done, g, nrstd_ready)
            steps(pool, NG, node_step, lag=1)

            for s in range(RING):
                hold(pool, x1_out[s], ((NG - 1 - s) // RING + 1) * DMA)
            for i in range(RING):
                gather(i, i, x1, K, edge_sums, gidx1_copied, gathered1)

            def edge_step1(i, s, _):
                scatter(i, s, msum, msg_ready, sidx1_copied, scattered1, None)
                if in_range(i + RING, NB):
                    gather(i + RING, s, x1, K, edge_sums, gidx1_copied, gathered1)
            for i in range(RING):
                edge_step1(i, i, 0)
            turns = (NB - RING) // RING
            with pool.Fori(1, turns) as j:
                for s in range(RING):
                    edge_step1(j * RING + s, s, j)
            for i in range(turns * RING, NB):
                edge_step1(i, i % RING, turns)

            def gru_step(g, s, j):
                c, b = (s - 1) % 2, (s - 1) % RING
                if in_range(g - 1, NG):
                    hold(pool, n_ready, g)
                    nc.gpsimd.tensor_tensor(hm_sb[:, c, :], xt1[:, b, :], n_sb[:, c, :], ALU.subtract)\
                        .then_inc(hm_ready, 1)
                    hold(pool, hm_ready, g)
                    hold(pool, z_ready, g)
                    nc.gpsimd.tensor_tensor(zh_sb[:, c, :], z_sb[:, c, :], hm_sb[:, c, :], ALU.mult)\
                        .then_inc(zh_ready, 1)
                    hold(pool, zh_ready, g)
                    hold(pool, back_done, g - 2)
                    nc.gpsimd.tensor_tensor(hf_sb[:, c, :], n_sb[:, c, :], zh_sb[:, c, :], ALU.add)\
                        .then_inc(hf_ready, 1)
                if in_range(g - 2, NG):
                    hold(pool, ymv_ready, g - 1)
                    inverse_std(s % 2, yeps_done, g - 1, yrstd_ready)
            steps(pool, NG, gru_step, lag=2)

        @block.tensor
        def _(pe):
            def mm(to, left, right, start=True, stop=True):
                return nc.tensor.matmul(to, left, right, start=start, stop=stop)

            pe.wait_ge(pool_set, 3)
            pe.wait_ge(rows_ready, 1)
            for n in range(4):
                for c in range(2):
                    at = (n // 2) * W + (n % 2) * TILES + c * HALF
                    last = nc.tensor.transpose(turned_ps[:, at:at + HALF], rows_f[0:HALF, n, c, :],
                                               ident[0:HALF, 0:HALF])
            last.then_inc(setup_turned, 1)
            pe.wait_ge(weights_in, WEIGHT_LOADS * DMA)
            nc.tensor.transpose(bank[2][:, 0:P], wmsg_raw[:, :], ident[:, :])
            for b in range(3):
                nc.tensor.transpose(bank[0][:, b * P:(b + 1) * P], wih_raw[:, b, :], ident[:, :])
            for b in range(3):
                last = nc.tensor.transpose(bank[1][:, b * P:(b + 1) * P], whh_raw[:, b, :], ident[:, :])
            last.then_inc(setup_turned, 1)
            pe.wait_ge(weights_ready, 1)
            pe.wait_ge(index_ready, 1)

            h1_ps, h1n_ps, h2_ps, sum_ps = bank[0], bank[1], bank[2], bank[3]

            def linear(ps, parts, bias_row):
                for k in range(K):
                    to = ps[:, k * P:(k + 1) * P]
                    for n, (left, right) in enumerate(parts):
                        mm(to, left[:, k * P:(k + 1) * P], right, start=(n == 0), stop=False)
                    last = mm(to, ones_row[0:1, :], bias_row[0:1, :], start=False)
                return last

            def edge_step(i, s, j):
                c = s % 2
                if in_range(i, NB):
                    wait(pe, gathered[s], (j + 1) * 2 * K * DMA)
                    wait(pe, xt_ready, i)
                    for k in range(2 * K):
                        last = nc.tensor.transpose(turned_ps[:, k * P:(k + 1) * P], xg[:, s, k, :], ident[:, :])
                    last.then_inc(xg_turned, 1)
                if in_range(i - 1, NB):
                    wait(pe, h1n_ready, i)
                    wait(pe, y1_ready, i - 1)
                    for k in range(K):
                        last = nc.tensor.transpose(h1n_ps[:, k * P:(k + 1) * P],
                                                   h1n[:, 1 - c, k * P:(k + 1) * P], ident[:, :])
                    last.then_inc(h1n_turned, 1)
                if in_range(i, NB):
                    wait(pe, xt_ready, i + 1)
                    wait(pe, h1n_ready, i)
                    linear(h1_ps, [(xt[:, c, 0:W], w1_sb[:, 0, :]), (xt[:, c, W:], w1_sb[:, 1, :])], b1_row)\
                        .then_inc(h1_done, 1)
                if in_range(i - 1, NB):
                    wait(pe, act1_ready, i)
                    wait(pe, h2n_ready, i - 1)
                    linear(h2_ps, [(act1[:, 1 - c, :], w2_sb[:, :])], b2_row).then_inc(h2_done, 1)
                if in_range(i - 2, NB):
                    wait(pe, hout_ready, i - 1)
                    wait(pe, equal_made, i - 1)
                    wait(pe, total_ready, i - 2)
                    for a in range(K):
                        for k in range(a, K):
                            last = mm(sum_ps[:, a * P:(a + 1) * P],
                                      equal[:, c, eq_at(k) + a * P:eq_at(k) + (a + 1) * P],
                                      hout[:, c, k * P:(k + 1) * P], start=(k == a), stop=(k == K - 1))
                    last.then_inc(sums_done, 1)
            steps(pe, NB, edge_step, lag=2)

            def edge_step1(i, s, j):
                c = s % 2
                if in_range(i, NB):
                    wait(pe, gathered1[s], (j + 1) * K * DMA)
                    wait(pe, equal1_made, i + 1)
                    wait(pe, at_ready, i - 1)
                    for k in reversed(range(K)):
                        n = (k + 1) * P
                        mm(bank[c][:, 0:n], xg[:, s, k, :], equal[:, c, eq_at(k):eq_at(k) + n],
                           start=(k == K - 1), stop=(k == 0))
                    for k in reversed(range(K)):
                        n = (k + 1) * P
                        last = mm(bank[2 + c][0:T_TYPES, 0:n], onehot[:, c, k, :],
                                  equal[:, c, eq_at(k):eq_at(k) + n], start=(k == K - 1), stop=(k == 0))
                    last.then_inc(edge_sums, 1)
                if in_range(i - 1, NB):
                    wait(pe, at_ready, i)
                    wait(pe, msg_ready, i - 1)
                    for a in range(K):
                        cols = slice(a * P, (a + 1) * P)
                        mm(bank[4][:, cols], at_sb[:, 1 - c, cols], wmsg_t[:, :], stop=False)
                        last = mm(bank[4][:, cols], ct_sb[:, 1 - c, cols], embb[:, :], start=False)
                    last.then_inc(msg_done, 1)
            steps(pe, NB, edge_step1, lag=1)

            r_ps, hn_ps, z_ps, in_ps, back_ps = bank[0], bank[1], bank[2], bank[3], bank[5]

            def gru_step(g, s, j):
                c = s % 2
                if in_range(g, NG):
                    wait(pe, s_in[s], (j + 1) * DMA)
                    wait(pe, mt_ready, g)
                    for k in range(K):
                        nc.tensor.transpose(turned_ps[:, k * P:(k + 1) * P], ng_s[:, s, k * P:(k + 1) * P],
                                            ident[:, :])
                    wait(pe, x1_in[s], (j + 1) * DMA)
                    wait(pe, xt1_ready, g)
                    for k in range(K):
                        last = nc.tensor.transpose(turned_ps[:, W + k * P:W + (k + 1) * P],
                                                   ng_x[:, s, k * P:(k + 1) * P], ident[:, :])
                    last.then_inc(g_turned, 1)
                if in_range(g - 1, NG):
                    m, h = mt[:, 1 - c, :], xt1[:, (s - 1) % RING, :]
                    wait(pe, mt_ready, g)
                    wait(pe, xt1_ready, g)
                    wait(pe, r_ready, g - 1)
                    mm(r_ps[:, :], wih_t[:, 0:P], m, stop=False)
                    mm(r_ps[:, :], whh_t[:, 0:P], h, start=False).then_inc(r_done, 1)
                    wait(pe, rh_ready, g - 1)
                    mm(hn_ps[:, :], whh_t[:, 2 * P:], h).then_inc(hn_done, 1)
                    wait(pe, pre_ready, g - 1)
                    mm(in_ps[:, :], wih_t[:, 2 * P:], m).then_inc(in_done, 1)
                    wait(pe, z_ready, g - 1)
                    mm(z_ps[:, :], wih_t[:, P:2 * P], m, stop=False)
                    mm(z_ps[:, :], whh_t[:, P:2 * P], h, start=False).then_inc(z_done, 1)
                if in_range(g - 2, NG):
                    wait(pe, hf_ready, g - 1)
                    wait(pe, y_ready, g - 2)
                    for k in range(K):
                        last = nc.tensor.transpose(back_ps[:, k * P:(k + 1) * P],
                                                   hf_sb[:, c, k * P:(k + 1) * P], ident[:, :])
                    last.then_inc(back_done, 1)
            steps(pe, NG, gru_step, lag=2)

        @block.scalar
        def _(act):
            h1n_ps, sum_ps = bank[1], bank[3]
            act.wait_ge(weights_ready, 1)

            def edge_step(i, s, j):
                c = s % 2
                if in_range(i, NB):
                    wait(act, xg_turned, i + 1)
                    wait(act, h1_done, i - 1)
                    nc.scalar.activation(xt[:, c, 0:W], turned_ps[:, 0:W], ACT.Copy)
                    nc.scalar.activation(xt[:, c, W:], turned_ps[:, W:], ACT.Copy).then_inc(xt_ready, 1)
                if in_range(i - 1, NB):
                    wait(act, h1n_turned, i)
                    wait(act, act1_ready, i - 2)
                    nc.scalar.activation(y1[:, 1 - c, :], h1n_ps[:, :], ACT.Identity, bias=be1_col[:, 0:1],
                                         scale=g1_col[:, 0:1]).then_inc(y1_ready, 1)
                if in_range(i, NB):
                    wait(act, mv1_ready, i + 1)
                    nc.scalar.activation(std[:, 0, :], mv[:, 0, :, 1], ACT.Sqrt, bias=eps_col[:, 0:1])\
                        .then_inc(std1_ready, 1)
                if in_range(i - 1, NB):
                    wait(act, mv2_ready, i)
                    nc.scalar.activation(std[:, 1, :], mv[:, 1, :, 1], ACT.Sqrt, bias=eps_col[:, 0:1])\
                        .then_inc(std2_ready, 1)
                if in_range(i - 2, NB):
                    wait(act, sums_done, i - 1)
                    wait(act, scattered, (i - 3) * K * DMA)
                    nc.scalar.activation(total[:, (s - 2) % RING, :], sum_ps[:, :], ACT.Copy)\
                        .then_inc(total_ready, 1)
            steps(act, NB, edge_step, lag=2)

            def store_x1(g, s, j):
                wait(act, x1_ready, g + 1)
                if isinstance(g, int) and g == NG - 1:
                    act.wait_ge(x1_out[(s - 1) % RING], ((g - 1) // RING + 1) * DMA)
                act.dma_start(group(x1, g), ng_x[:, s, :]).then_inc(x1_out[s], DMA)
            steps(act, NG, store_x1)

            def edge_step1(i, s, j):
                c = s % 2
                if in_range(i, NB):
                    wait(act, edge_sums, i + 1)
                    wait(act, msg_done, i - 1)
                    nc.scalar.activation(at_sb[:, c, :], bank[c][:, :], ACT.Copy)
                    nc.scalar.activation(ct_sb[:, c, :], bank[2 + c][0:T_TYPES, :], ACT.Copy).then_inc(at_ready, 1)
                if in_range(i - 1, NB):
                    wait(act, msg_done, i)
                    wait(act, scattered1, (i - 3) * K * DMA)
                    nc.scalar.activation(total[:, (s - 1) % RING, :], bank[4][:, :], ACT.Copy)\
                        .then_inc(msg_ready, 1)
            steps(act, NB, edge_step1, lag=1)

            r_ps, z_ps = bank[0], bank[2]

            def gru_step(g, s, j):
                c = s % 2
                if in_range(g, NG):
                    wait(act, g_turned, g + 1)
                    wait(act, in_done, g - 1)
                    wait(act, z_done, g - 1)
                    nc.scalar.activation(mt[:, c, :], turned_ps[:, 0:W], ACT.Copy).then_inc(mt_ready, 1)
                    wait(act, hm_ready, g - RING + 1)
                    nc.scalar.activation(xt1[:, s, :], turned_ps[:, W:], ACT.Copy).then_inc(xt1_ready, 1)
                if in_range(g - 1, NG):
                    wait(act, r_done, g)
                    wait(act, rh_ready, g - 2)
                    nc.scalar.activation(r_sb[:, 1 - c, :], r_ps[:, :], ACT.Sigmoid, bias=brz_col[:, 0:1])\
                        .then_inc(r_ready, 1)
                    wait(act, z_done, g)
                    wait(act, zh_ready, g - 2)
                    nc.scalar.activation(z_sb[:, 1 - c, :], z_ps[:, :], ACT.Sigmoid, bias=brz_col[:, 1:2])\
                        .then_inc(z_ready, 1)
                    wait(act, pre_ready, g)
                    wait(act, hf_ready, g - 2)
                    nc.scalar.activation(n_sb[:, 1 - c, :], pre_n[:, 1 - c, :], ACT.Tanh, bias=bih_col[:, 2:3])\
                        .then_inc(n_ready, 1)
                if in_range(g - 3, NG):
                    wait(act, o_ready, g - 2)
                    if isinstance(g, int) and g - 3 == NG - 1:
                        act.wait_ge(out_done[(s - 4) % RING], ((g - 4) // RING + 1) * DMA)
                    act.dma_start(group(out, g - 3), o_sb[:, (s - 3) % RING, :]).then_inc(out_done[(s - 3) % RING], DMA)
            steps(act, NG, gru_step, lag=3)
            for s in range(RING):
                act.wait_ge(out_done[s], ((NG - 1 - s) // RING + 1) * DMA)

        @block.vector
        def _(dve):
            nc.vector.memset(zeros[:, :], 0.0)
            nc.vector.memset(eps_col[:, :], EPS)
            nc.vector.memset(ones_row[:, :], 1.0).then_inc(cols_made, 1)
            dve.wait_ge(edges_in, EDGE_LOADS * DMA)
            nc.vector.tensor_copy(rows_f[0:HALF, 0:3], rows_i[0:HALF]).then_inc(rows_ready, 1)
            dve.wait_ge(setup_turned, 1)
            dve.wait_ge(pool_set, 7)

            def turned(n):
                at = (n // 2) * W + (n % 2) * TILES
                return turned_ps[:, at:at + TILES].rearrange("p (b k) -> p b k", k=K)

            nc.vector.tensor_copy(gather_idx[:, :, 0:K], turned(0))
            nc.vector.tensor_scalar(gather_idx[:, :, K:], turned(1), float(N - 1), None, ALU.min)
            nc.vector.tensor_copy(dst_col[:, :, :], turned(1)).then_inc(cols_made, 1)
            nc.vector.tensor_scalar(type_col[:, :, :], turned(2), 0.0, float(T_TYPES - 1), ALU.max, ALU.min)
            nc.vector.tensor_copy(w_col[:, :, :], turned(3))
            dve.wait_ge(cols_made, 2)
            nc.vector.tensor_tensor(to_spill[:, :, :], spill_row[:, :, :], dst_col[:, :, :], ALU.subtract)\
                .then_inc(index_ready, 1)
            dve.wait_ge(setup_turned, 2)
            nc.vector.tensor_copy(wmsg_t[:, :], bank[2][:, 0:P])
            nc.vector.tensor_copy(wih_t[:, :], bank[0][:, 0:3 * P])
            nc.vector.tensor_copy(whh_t[:, :], bank[1][:, 0:3 * P])
            nc.vector.tensor_tensor(brz_col[:, :], bih_col[:, 0:2], bhh_col[:, 0:2], ALU.add)
            nc.vector.tensor_tensor(embb[:, :], emb_sb[:, :], bmsg_all[:, :], ALU.add).then_inc(weights_ready, 1)
            dve.wait_ge(index_ready, 1)

            h1_ps, h2_ps = bank[0], bank[2]

            def equalities(i, c, weighted, made, ready):
                for k in range(K):
                    n = (k + 1) * P
                    last = nc.vector.tensor_scalar(
                        equal[:, c, eq_at(k):eq_at(k) + n], dst_row[:, c, 0:n], dst_col[:, i, k:k + 1],
                        w_col[:, i, k:k + 1] if weighted else None, ALU.is_equal,
                        ALU.mult if weighted else ALU.bypass)
                last.then_inc(made, 1)

            def row_stats(ps, to_stats, to_mv, done, value, ready):
                for k in range(K):
                    last = nc.vector.bn_stats(to_stats[:, k, :], ps[:, k * P:(k + 1) * P])
                last.then_inc(done, 1)
                hold(dve, done, value)
                for k in range(K):
                    last = nc.vector.bn_aggr(to_mv[:, k, :], to_stats[:, k, :])
                last.then_inc(ready, 1)

            def normalise(to, ps, means, scales, ready):
                for k in range(K):
                    last = nc.vector.tensor_scalar(to[:, k * P:(k + 1) * P], ps[:, k * P:(k + 1) * P],
                                                   means[:, k, 0:1], scales[:, k:k + 1], ALU.subtract, ALU.mult)
                last.then_inc(ready, 1)

            def every_tile(row):
                return row[:, None, :].to_broadcast([P, K, P])

            def tiles(a):
                return a.rearrange("p (k f) -> p k f", k=K)

            def edge_step(i, s, j):
                c = s % 2
                if in_range(i - 2, NB):
                    b = i - 2
                    half = j - 1 if s < 2 else j
                    wait(dve, dstrow_in[c], (2 * j + s // 2 - 1 + 1) * DMA)
                    wait(dve, sums_done, b - 1)
                    equalities(b, c, True, equal_made, None)
                    wait(dve, sidx_made, b - 1)
                    for k in range(K):
                        n = (k + 1) * P
                        last = nc.vector.scalar_tensor_tensor(
                            out=junk[:, k, 0:n], in0=dst_row[:, c, 0:n], scalar=dst_col[:, b, k:k + 1],
                            in1=before[:, W - n:], op0=ALU.is_equal, op1=ALU.mult, accum_out=dups[:, c, k:k + 1])
                    last.then_inc(dup_done, 1)
                    wait(dve, dup_done, b + 1)
                    nc.vector.scalar_tensor_tensor(out=moved[:, c, :], in0=dups[:, c, :], scalar=0.0,
                                                   in1=to_spill[:, b, :], op0=ALU.is_gt, op1=ALU.mult)\
                        .then_inc(moved_done, 1)
                    wait(dve, moved_done, b + 1)
                    nc.vector.tensor_tensor(scatter_idx[:, b, :], moved[:, c, :], dst_col[:, b, :], ALU.add)\
                        .then_inc(sidx_made, 1)
                if in_range(i - 1, NB):
                    wait(dve, y1_ready, i)
                    wait(dve, h2_done, i - 2)
                    nc.vector.scalar_tensor_tensor(out=act1[:, 1 - c, :], in0=y1[:, 1 - c, :], scalar=SLOPE,
                                                   in1=y1[:, 1 - c, :], op0=ALU.mult, op1=ALU.max)\
                        .then_inc(act1_ready, 1)
                if in_range(i, NB):
                    wait(dve, h1_done, i + 1)
                    wait(dve, std1_ready, i)
                    row_stats(h1_ps, stats[:, 0], mv[:, 0], st1_done, i + 1, mv1_ready)
                    wait(dve, std1_ready, i + 1)
                    nc.vector.reciprocal(rstd[:, 0, :], std[:, 0, :]).then_inc(rstd1_ready, 1)
                    wait(dve, rstd1_ready, i + 1)
                    wait(dve, h1n_turned, i - 1)
                    normalise(h1n[:, c, :], h1_ps, mv[:, 0], rstd[:, 0, :], h1n_ready)
                if in_range(i - 1, NB):
                    wait(dve, h2_done, i)
                    row_stats(h2_ps, stats[:, 1], mv[:, 1], st2_done, i, mv2_ready)
                    wait(dve, std2_ready, i)
                    nc.vector.reciprocal(rstd[:, 1, :], std[:, 1, :]).then_inc(rstd2_ready, 1)
                    wait(dve, rstd2_ready, i)
                    normalise(h2n[:, :], h2_ps, mv[:, 1], rstd[:, 1, :], h2n_ready)
                    wait(dve, h2n_ready, i)
                    nc.vector.tensor_tensor(tiles(h2g[:, :]), tiles(h2n[:, :]), every_tile(g2_all), ALU.mult)\
                        .then_inc(h2g_ready, 1)
                    wait(dve, h2g_ready, i)
                    nc.vector.tensor_tensor(tiles(h2b[:, :]), tiles(h2g[:, :]), every_tile(be2_all), ALU.add)\
                        .then_inc(h2b_ready, 1)
                    wait(dve, h2b_ready, i)
                    wait(dve, sums_done, i - 2)
                    nc.vector.scalar_tensor_tensor(out=hout[:, 1 - c, :], in0=h2b[:, :], scalar=SLOPE,
                                                   in1=h2b[:, :], op0=ALU.mult, op1=ALU.max)\
                        .then_inc(hout_ready, 1)
            steps(dve, NB, edge_step, lag=2)

            def node_step(g, s, j):
                if in_range(g, NG):
                    wait(dve, res_ready, g + 1)
                    wait(dve, nrstd_ready, g - 1)
                    row_stats(ng_s[:, s], n_stats[:, s % 2], n_mv[:, s % 2], nst_done, g + 1, nmv_ready)
                if in_range(g - 1, NG):
                    wait(dve, nrstd_ready, g)
                    normalise(ng_x[:, (s - 1) % RING], ng_s[:, (s - 1) % RING], n_mv[:, (s - 1) % 2],
                              n_rstd[:, (s - 1) % 2], x1_ready)
            steps(dve, NG, node_step, lag=1)

            def edge_step1(i, s, j):
                c = s % 2
                wait(dve, dstrow1_in[c], (2 * j + s // 2 + 1) * DMA)
                wait(dve, edge_sums, i - 1)
                nc.vector.tensor_tensor(
                    onehot[:, c], type_col[:, i, :].rearrange("p (k a) -> p k a", a=1).to_broadcast([P, K, T_TYPES]),
                    type_no[:, None, :].to_broadcast([P, K, T_TYPES]), ALU.is_equal)
                equalities(i, c, False, equal1_made, None)
            steps(dve, NB, edge_step1)

            hn_ps, in_ps, back_ps = bank[1], bank[3], bank[5]

            def gru_step(g, s, j):
                c = s % 2
                if in_range(g - 1, NG):
                    wait(dve, hn_done, g)
                    wait(dve, r_ready, g)
                    wait(dve, pre_ready, g - 2)
                    nc.vector.scalar_tensor_tensor(out=rh_sb[:, 1 - c, :], in0=hn_ps[:, :], scalar=bhh_col[:, 2:3],
                                                   in1=r_sb[:, 1 - c, :], op0=ALU.add, op1=ALU.mult)\
                        .then_inc(rh_ready, 1)
                    wait(dve, rh_ready, g)
                    wait(dve, in_done, g)
                    wait(dve, n_ready, g - 2)
                    nc.vector.tensor_tensor(pre_n[:, 1 - c, :], rh_sb[:, 1 - c, :], in_ps[:, :], ALU.add)\
                        .then_inc(pre_ready, 1)
                if in_range(g - 2, NG):
                    wait(dve, back_done, g - 1)
                    nc.vector.tensor_tensor(y_sb[:, c, :], back_ps[:, :], ng_x[:, (s - 2) % RING, :], ALU.add)\
                        .then_inc(y_ready, 1)
                    wait(dve, y_ready, g - 1)
                    row_stats(y_sb[:, c], n_stats[:, c], n_mv[:, c], yst_done, g - 1, ymv_ready)
                    wait(dve, yrstd_ready, g - 1)
                    normalise(o_sb[:, (s - 2) % RING], y_sb[:, c], n_mv[:, c], n_rstd[:, c], o_ready)
            steps(dve, NG, gru_step, lag=2)


EDGE_LOADS = 12
WEIGHT_LOADS = 15

_INS = ['x', 'src', 'dst', 'edge_type_9', 'edge_weight', 'L0_gnn_w1', 'L0_gnn_b1', 'L0_gnn_g1', 'L0_gnn_be1',
        'L0_gnn_w2', 'L0_gnn_b2', 'L0_gnn_g2', 'L0_gnn_be2', 'L1_gnn_W_msg', 'L1_gnn_b_msg', 'L1_gnn_edge_embed',
        'L1_gnn_W_ih', 'L1_gnn_W_hh', 'L1_gnn_b_ih', 'L1_gnn_b_hh']


def kernel(**inputs):
    import numpy as _np
    import concourse.bacc as _bacc
    from concourse import mybir as _mybir
    from concourse.bass_utils import run_bass_kernel_spmd as _run

    nc = _bacc.Bacc("TRN2", target_bir_lowering=False, num_devices=1)
    arrays, args = {}, []
    for name in _INS:
        a = _np.ascontiguousarray(inputs[name])
        arrays[f"in_{name}"] = a
        args.append(nc.dram_tensor(f"in_{name}", a.shape, _mybir.dt.from_np(a.dtype), kind="ExternalInput").ap())
    shape = inputs['x'].shape
    args.append(nc.dram_tensor("out_0", shape, _mybir.dt.float32, kind="ExternalOutput").ap())
    gnn_kernel(nc, *args)
    r = _run(nc, [arrays], core_ids=[0])
    return r.results[0]["out_0"]
```

```python
from contextlib import ExitStack

import concourse.bass as bass
from concourse import mybir

F32 = mybir.dt.float32
I32 = mybir.dt.int32
ALU = mybir.AluOpType
ACT = mybir.ActivationFunctionType

P = 128
K = 4
W = K * P
RING = 4
EPS = 1e-5
SLOPE = 0.2
DMA = 16


def gnn_kernel(nc, x, src, dst, edge_type, edge_weight, w1, b1, g1, be1, w2, b2, g2, be2,
               W_msg, b_msg, edge_embed, W_ih, W_hh, b_ih, b_hh, out):
    N, H = x.shape
    E = src.shape[0]
    T_TYPES = edge_embed.shape[0]
    NB = -(-E // W)
    TILES = NB * K
    HALF = TILES // 2
    FULL_G = N // W
    NG = FULL_G + 1
    ROWS = -(-(N + W) // (16 * P)) * 16 * P
    ZCOLS = 2048
    ZCHUNKS = ROWS * H // (P * ZCOLS)
    assert H == P and TILES == 2 * HALF and HALF <= P and ZCHUNKS * ZCOLS * P == ROWS * H
    whole_rows = E // P - HALF
    rest = E - (E // P) * P
    assert rest and whole_rows == HALF - 1
    PAD_TARGET = N + (K - 1) * P

    def eq_at(k):
        return P * k * (k + 1) // 2

    agg = nc.dram_tensor("agg", [ROWS, H], F32, kind="Internal").ap()
    msum = nc.dram_tensor("msum", [ROWS, H], F32, kind="Internal").ap()
    x1 = nc.dram_tensor("x1", [N, H], F32, kind="Internal").ap()
    dpad = nc.dram_tensor("dpad", [NB, W], I32, kind="Internal").ap()

    def groups(t):
        return (t[0:FULL_G * W, :].rearrange("(g p j) f -> g p (j f)", p=P, j=K),
                t[N - W:N, :].rearrange("(p j) f -> p (j f)", p=P))

    def zero_chunk(t, z):
        return t.rearrange("(p r) f -> p (r f)", p=P).rearrange("p (z c) -> z p c", c=ZCOLS)[z]

    def group(t, g):
        whole, last = groups(t)
        return last if isinstance(g, int) and g == NG - 1 else whole[g]

    ctx = ExitStack()
    with ctx:
        def sb(name, shape, dt=F32):
            return ctx.enter_context(nc.sbuf_tensor(name, shape, dt))

        def sem(name):
            return ctx.enter_context(nc.semaphore(name))

        def sem_ring(name):
            return [sem(f"{name}{s}") for s in range(RING)]

        bank = [ctx.enter_context(nc.psum_tensor(f"bank{b}", [P, W], F32)) for b in range(6)]
        turned_ps = ctx.enter_context(nc.psum_tensor("turned_ps", [P, 2 * W], F32))

        ident = sb("ident", [P, P])
        before = sb("before", [P, W])
        zeros = sb("zeros", [P, ZCOLS])
        eps_col = sb("eps_col", [P, 1])
        w1_sb = sb("w1_sb", [P, 2, P])
        w2_sb = sb("w2_sb", [P, P])
        b1_col = sb("b1_col", [P, 1])
        b2_col = sb("b2_col", [P, 1])
        g1_col = sb("g1_col", [P, 1])
        be1_col = sb("be1_col", [P, 1])
        g2_all = sb("g2_all", [P, P])
        be2_all = sb("be2_all", [P, P])
        wmsg_raw = sb("wmsg_raw", [P, P])
        wih_raw = sb("wih_raw", [P, 3, P])
        whh_raw = sb("whh_raw", [P, 3, P])
        wmsg_t = sb("wmsg_t", [P, P])
        wih_t = sb("wih_t", [P, 3 * P])
        whh_t = sb("whh_t", [P, 3 * P])
        bih_col = sb("bih_col", [P, 3])
        bhh_col = sb("bhh_col", [P, 3])
        brz_col = sb("brz_col", [P, 2])
        emb_sb = sb("emb_sb", [T_TYPES, P])
        bmsg_all = sb("bmsg_all", [T_TYPES, P])
        embb = sb("embb", [T_TYPES, P])
        type_no = sb("type_no", [P, T_TYPES])
        rows_i = sb("rows_i", [P, 3, 2, P], I32)
        rows_f = sb("rows_f", [P, 4, 2, P])
        gather_idx = sb("gather_idx", [P, NB, 2 * K], I32)
        scatter_idx = sb("scatter_idx", [P, NB, K], I32)
        dst_col = sb("dst_col", [P, NB, K])
        spill_row = sb("spill_row", [P, NB, K], I32)
        to_spill = sb("to_spill", [P, NB, K])
        type_col = sb("type_col", [P, NB, K])
        w_col = sb("w_col", [P, NB, K])
        gidx_slot = sb("gidx_slot", [P, RING, 2 * K], I32)
        sidx_slot = sb("sidx_slot", [P, RING, K], I32)
        xg = sb("xg", [P, RING, 2 * K, P])
        dst_row = sb("dst_row", [P, 2, W], I32)
        equal = sb("equal", [P, 2, eq_at(K)])
        junk = sb("junk", [P, K, W])
        dups = sb("dups", [P, 2, K])
        moved = sb("moved", [P, 2, K])
        xt = sb("xt", [P, 2, 2 * W])
        h1n = sb("h1n", [P, 2, W])
        y1 = sb("y1", [P, 2, W])
        act1 = sb("act1", [P, 2, W])
        h1t_sb = sb("h1t_sb", [P, W])
        h2t_sb = sb("h2t_sb", [P, W])
        sumt_sb = sb("sumt_sb", [P, W])
        msgt_sb = sb("msgt_sb", [P, W])
        h2n = sb("h2n", [P, W])
        h2g = sb("h2g", [P, W])
        h2b = sb("h2b", [P, W])
        hout = sb("hout", [P, 2, W])
        total = sb("total", [P, RING, W])
        stats = sb("stats", [P, 2, K, 6])
        mv = sb("mv", [P, 2, K, 2])
        std = sb("std", [P, 2, K])
        rstd = sb("rstd", [P, 2, K])
        shift = sb("shift", [P, 2, K])
        onehot = sb("onehot", [P, 2, K, T_TYPES])
        at_sb = sb("at_sb", [P, 2, W])
        ct_sb = sb("ct_sb", [T_TYPES, 2, W])
        ng_x = sb("ng_x", [P, RING, W])
        ng_s = sb("ng_s", [P, RING, W])
        n_stats = sb("n_stats", [P, 2, K, 6])
        n_mv = sb("n_mv", [P, 2, K, 2])
        n_shift = sb("n_shift", [P, 2, K])
        n_var = sb("n_var", [P, 2, K])
        minus_half = sb("minus_half", [P, K])
        n_rstd = sb("n_rstd", [P, 2, K])
        mt = sb("mt", [P, 2, W])
        xt1 = sb("xt1", [P, RING, W])
        r_sb = sb("r_sb", [P, 2, W])
        z_sb = sb("z_sb", [P, 2, W])
        rh_sb = sb("rh_sb", [P, 2, W])
        pre_n = sb("pre_n", [P, 2, W])
        n_sb = sb("n_sb", [P, 2, W])
        zn_sb = sb("zn_sb", [P, 2, W])
        zh_sb = sb("zh_sb", [P, 2, W])
        hf_sb = sb("hf_sb", [P, 2, W])
        y_sb = sb("y_sb", [P, 2, W])
        ng_o = sb("ng_o", [P, RING, W])

        pool_set = sem("pool_set")
        pads_set = sem("pads_set")
        edges_in = sem("edges_in")
        weights_in = sem("weights_in")
        rows_ready = sem("rows_ready")
        setup_turned = sem("setup_turned")
        weights_ready = sem("weights_ready")
        cols_made = sem("cols_made")
        index_ready = sem("index_ready")
        dpad_out = sem("dpad_out")
        agg_zeroed = sem("agg_zeroed")
        msum_zeroed = sem("msum_zeroed")
        passed = sem("passed")
        gidx_copied = sem("gidx_copied")
        sidx_copied = sem("sidx_copied")
        gathered = sem_ring("gathered")
        dstrow_in = [sem("dstrow_in0"), sem("dstrow_in1")]
        equal_made = sem("equal_made")
        dup_done = sem("dup_done")
        moved_done = sem("moved_done")
        sidx_made = sem("sidx_made")
        xg_turned = sem("xg_turned")
        xt_ready = sem("xt_ready")
        h1_done = sem("h1_done")
        st1_done = sem("st1_done")
        mv1_ready = sem("mv1_ready")
        std1_ready = sem("std1_ready")
        rstd1_ready = sem("rstd1_ready")
        shift1_ready = sem("shift1_ready")
        h1n_ready = sem("h1n_ready")
        h1n_turned = sem("h1n_turned")
        y1_ready = sem("y1_ready")
        act1_ready = sem("act1_ready")
        h1t_ready = sem("h1t_ready")
        h1_back = sem("h1_back")
        h2_done = sem("h2_done")
        h2t_ready = sem("h2t_ready")
        h2_back = sem("h2_back")
        shift2_ready = sem("shift2_ready")
        st2_done = sem("st2_done")
        mv2_ready = sem("mv2_ready")
        std2_ready = sem("std2_ready")
        rstd2_ready = sem("rstd2_ready")
        h2n_ready = sem("h2n_ready")
        h2g_ready = sem("h2g_ready")
        h2b_ready = sem("h2b_ready")
        hout_ready = sem("hout_ready")
        sums_done = sem("sums_done")
        sumt_ready = sem("sumt_ready")
        sums_back = sem("sums_back")
        total_ready = sem("total_ready")
        scattered = sem("scattered")
        x_in = sem_ring("x_in")
        agg_in = sem_ring("agg_in")
        res_ready = sem("res_ready")
        nst_done = sem("nst_done")
        nmv_ready = sem("nmv_ready")
        nstd_ready = sem("nstd_ready")
        nshift_ready = sem("nshift_ready")
        nrstd_ready = sem("nrstd_ready")
        x1_ready = sem("x1_ready")
        x1_out = sem_ring("x1_out")
        gidx1_copied = sem("gidx1_copied")
        sidx1_copied = sem("sidx1_copied")
        gathered1 = sem_ring("gathered1")
        dstrow1_in = [sem("dstrow1_in0"), sem("dstrow1_in1")]
        equal1_made = sem("equal1_made")
        edge_sums = sem("edge_sums")
        at_ready = sem("at_ready")
        msg_done = sem("msg_done")
        msgt_ready = sem("msgt_ready")
        msg_back = sem("msg_back")
        msg_ready = sem("msg_ready")
        scattered1 = sem("scattered1")
        s_in = sem_ring("s_in")
        x1_in = sem_ring("x1_in")
        g_turned = sem("g_turned")
        mt_ready = sem("mt_ready")
        xt1_ready = sem("xt1_ready")
        r_done = sem("r_done")
        hn_done = sem("hn_done")
        z_done = sem("z_done")
        in_done = sem("in_done")
        r_ready = sem("r_ready")
        z_ready = sem("z_ready")
        rh_ready = sem("rh_ready")
        pre_ready = sem("pre_ready")
        n_ready = sem("n_ready")
        zn_ready = sem("zn_ready")
        zh_ready = sem("zh_ready")
        hf_ready = sem("hf_ready")
        back_done = sem("back_done")
        y_ready = sem("y_ready")
        yst_done = sem("yst_done")
        ymv_ready = sem("ymv_ready")
        yeps_done = sem("yeps_done")
        yrstd_ready = sem("yrstd_ready")
        o_ready = sem("o_ready")
        out_done = sem_ring("out_done")

        def steps(eng, count, step, lag=0):
            for i in range(RING):
                step(i, i, 0)
            turns = count // RING
            with eng.Fori(1, turns) as j:
                for s in range(RING):
                    step(j * RING + s, s, j)
            for i in range(turns * RING, count + lag):
                step(i, i % RING, i // RING)

        def in_range(i, n):
            return not isinstance(i, int) or 0 <= i < n

        def used(count):
            return max(count, 0) if isinstance(count, int) else count

        block = ctx.enter_context(nc.Block())

        @block.sync
        def _(sp):
            sp.wait_ge(pads_set, 4)
            sp.sem_inc(passed, 1)
            edge_loads = 0
            whole = HALF * P
            for n, a in enumerate((src, dst, edge_type, edge_weight)):
                to = rows_i[:, n] if n < 3 else rows_f[:, 3]
                sp.dma_start(to[0:HALF, 0, :], a[0:whole].rearrange("(q e) -> q e", e=P)).then_inc(edges_in, DMA)
                sp.dma_start(to[0:whole_rows, 1, :],
                             a[whole:whole + whole_rows * P].rearrange("(q e) -> q e", e=P)).then_inc(edges_in, DMA)
                sp.dma_start(to[whole_rows:HALF, 1, 0:rest],
                             a[E - rest:E].rearrange("(q e) -> q e", q=1)).then_inc(edges_in, DMA)
                edge_loads += 3
            with nc.allow_non_contiguous_dma(reason="columns of a few hundred bytes"):
                loads = [
                    (w1_sb[:, :, :], w1.rearrange("(h k) n -> k h n", h=2)), (w2_sb[:, :], w2),
                    (b1_col[:, :], b1.rearrange("(n a) -> n a", a=1)), (b2_col[:, :], b2.rearrange("(n a) -> n a", a=1)),
                    (g1_col[:, :], g1.rearrange("(n a) -> n a", a=1)), (be1_col[:, :], be1.rearrange("(n a) -> n a", a=1)),
                    (g2_all[:, :], g2.partition_broadcast(P)), (be2_all[:, :], be2.partition_broadcast(P)),
                    (wmsg_raw[:, :], W_msg), (wih_raw[:, :, :], W_ih.rearrange("(b p) k -> p b k", b=3)),
                    (whh_raw[:, :, :], W_hh.rearrange("(b p) k -> p b k", b=3)),
                    (bih_col[:, :], b_ih.rearrange("(b p) -> p b", b=3)), (bhh_col[:, :], b_hh.rearrange("(b p) -> p b", b=3)),
                    (emb_sb[:, :], edge_embed), (bmsg_all[:, :], b_msg.partition_broadcast(T_TYPES)),
                ]
                assert len(loads) == WEIGHT_LOADS and edge_loads == EDGE_LOADS
                for to, a in loads:
                    sp.dma_start(to, a).then_inc(weights_in, DMA)
            sp.wait_ge(edges_in, EDGE_LOADS * DMA)
            sp.sem_inc(passed, 1)
            sp.dma_start(dpad.rearrange("b w -> (b w)").rearrange("(c q e) -> q c e", c=2, e=P),
                         rows_i[0:HALF, 1]).then_inc(dpad_out, DMA)
            sp.wait_ge(cols_made, 1)
            sp.sem_inc(passed, 1)
            sp.wait_ge(dpad_out, DMA)
            sp.sem_inc(passed, 1)

            def load_targets(i, s, j):
                sp.wait_ge(sidx_made, used(i - 1))
                sp.sem_inc(passed, 1)
                sp.dma_start(dst_row[:, s % 2, :], dpad[i].partition_broadcast(P))\
                    .then_inc(dstrow_in[s % 2], DMA)
                if s % 2 and (not isinstance(i, int) or i // 2 < ZCHUNKS):
                    sp.dma_start(zero_chunk(msum, 2 * j + s // 2), zeros[:, :]).then_inc(msum_zeroed, DMA)
            steps(sp, NB, load_targets)
            for z in range(NB // 2, ZCHUNKS):
                sp.dma_start(zero_chunk(msum, z), zeros[:, :]).then_inc(msum_zeroed, DMA)

            sp.wait_ge(scattered, NB * K * DMA)
            sp.sem_inc(passed, 1)

            def load_nodes(g, s, j):
                sp.wait_ge(x1_ready, used(g - RING + 1))
                sp.sem_inc(passed, 1)
                sp.dma_start(ng_x[:, s, :], group(x, g)).then_inc(x_in[s], DMA)
                sp.dma_start(ng_s[:, s, :], group(agg, g)).then_inc(agg_in[s], DMA)
            steps(sp, NG, load_nodes)

            def load_targets1(i, s, _):
                sp.wait_ge(equal1_made, used(i - 1))
                sp.sem_inc(passed, 1)
                sp.dma_start(dst_row[:, s % 2, :], dpad[i].partition_broadcast(P))\
                    .then_inc(dstrow1_in[s % 2], DMA)
            steps(sp, NB, load_targets1)

            sp.wait_ge(scattered1, NB * K * DMA)
            sp.sem_inc(passed, 1)

            def load_nodes1(g, s, j):
                sp.wait_ge(g_turned, used(g - RING + 1))
                sp.sem_inc(passed, 1)
                sp.dma_start(ng_s[:, s, :], group(msum, g)).then_inc(s_in[s], DMA)
                sp.wait_ge(y_ready, used(g - RING + 1))
                sp.sem_inc(passed, 1)
                sp.dma_start(ng_x[:, s, :], group(x1, g)).then_inc(x1_in[s], DMA)
            steps(sp, NG, load_nodes1)

        @block.gpsimd
        def _(pool):
            nc.gpsimd.memset(rows_i[:, 0], 0).then_inc(pads_set, 1)
            nc.gpsimd.iota(rows_i[:, 1], [[0, 2], [1, P]], base=PAD_TARGET, channel_multiplier=0).then_inc(pads_set, 1)
            nc.gpsimd.memset(rows_i[:, 2], 0).then_inc(pads_set, 1)
            nc.gpsimd.memset(rows_f[:, 3], 0.0).then_inc(pads_set, 1)
            nc.gpsimd.memset(ident[:, :], 0.0).then_inc(pool_set, 1)
            nc.gpsimd.memset(before[:, :], 1.0).then_inc(pool_set, 1)
            pool.wait_ge(pool_set, 2)
            nc.gpsimd.affine_select(out=ident[:, :], in_=ident[:, :], compare_op=ALU.not_equal, fill=1.0, base=0,
                                    pattern=[[-1, P]], channel_multiplier=1).then_inc(pool_set, 1)
            nc.gpsimd.affine_select(out=before[:, W - P:], in_=before[:, W - P:], compare_op=ALU.is_gt, fill=0.0,
                                    base=0, pattern=[[-1, P]], channel_multiplier=1).then_inc(pool_set, 1)
            nc.gpsimd.iota(spill_row[:, :, :], [[0, NB], [P, K]], base=N, channel_multiplier=1).then_inc(pool_set, 1)
            nc.gpsimd.memset(minus_half[:, :], -0.5).then_inc(pool_set, 1)
            nc.gpsimd.iota(type_no[:, :], [[1, T_TYPES]], base=0, channel_multiplier=0,
                           allow_small_or_imprecise_dtypes=True).then_inc(pool_set, 1)

            def scatter(i, s, table, values_ready, copied, done, indices_ready):
                if indices_ready is not None:
                    pool.wait_ge(indices_ready, i + 1)
                    pool.sem_inc(passed, 1)
                nc.gpsimd.tensor_copy(sidx_slot[:, s, :], scatter_idx[:, i, :]).then_inc(copied, 1)
                pool.wait_ge(copied, i + 1)
                pool.sem_inc(passed, 1)
                pool.wait_ge(values_ready, i + 1)
                pool.sem_inc(passed, 1)
                pool.wait_ge(done, used(i * K * DMA))
                pool.sem_inc(passed, 1)
                for k in range(K):
                    nc.gpsimd.indirect_dma_start(
                        table, bass.IndirectOffsetOnAxis(ap=sidx_slot[:, s, k:k + 1], axis=0),
                        total[:, s, k * P:(k + 1) * P], None, compute_op=ALU.add).then_inc(done, DMA)

            def gather(i, s, table, width, slot_free, copied, done):
                pool.wait_ge(slot_free, used(i - RING + 1))
                pool.sem_inc(passed, 1)
                nc.gpsimd.tensor_copy(gidx_slot[:, s, 0:width], gather_idx[:, i, 0:width]).then_inc(copied, 1)
                pool.wait_ge(copied, i + 1)
                pool.sem_inc(passed, 1)
                for k in range(width):
                    nc.gpsimd.indirect_dma_start(
                        xg[:, s, k, :], None, table,
                        bass.IndirectOffsetOnAxis(ap=gidx_slot[:, s, k:k + 1], axis=0)).then_inc(done[s], DMA)

            pool.wait_ge(index_ready, 1)
            pool.sem_inc(passed, 1)
            for i in range(RING):
                gather(i, i, x, 2 * K, xg_turned, gidx_copied, gathered)
            pool.wait_ge(agg_zeroed, ZCHUNKS * DMA)
            pool.sem_inc(passed, 1)

            def edge_step(i, s, _):
                scatter(i, s, agg, total_ready, sidx_copied, scattered, sidx_made)
                if in_range(i + RING, NB):
                    gather(i + RING, s, x, 2 * K, xg_turned, gidx_copied, gathered)
            for i in range(RING):
                edge_step(i, i, 0)
            turns = (NB - RING) // RING
            with pool.Fori(1, turns) as j:
                for s in range(RING):
                    edge_step(j * RING + s, s, j)
            for i in range(turns * RING, NB):
                edge_step(i, i % RING, turns)

            def node_step(g, s, j):
                pool.wait_ge(x_in[s], (j + 1) * DMA)
                pool.sem_inc(passed, 1)
                pool.wait_ge(agg_in[s], (j + 1) * DMA)
                pool.sem_inc(passed, 1)
                nc.gpsimd.tensor_tensor(ng_s[:, s, :], ng_s[:, s, :], ng_x[:, s, :], ALU.add)\
                    .then_inc(res_ready, 1)
            steps(pool, NG, node_step)

            pool.wait_ge(msum_zeroed, ZCHUNKS * DMA)
            pool.sem_inc(passed, 1)
            for s in range(RING):
                pool.wait_ge(x1_out[s], ((NG - 1 - s) // RING + 1) * DMA)
                pool.sem_inc(passed, 1)
            for i in range(RING):
                gather(i, i, x1, K, edge_sums, gidx1_copied, gathered1)

            def edge_step1(i, s, _):
                scatter(i, s, msum, msg_ready, sidx1_copied, scattered1, None)
                if in_range(i + RING, NB):
                    gather(i + RING, s, x1, K, edge_sums, gidx1_copied, gathered1)
            for i in range(RING):
                edge_step1(i, i, 0)
            turns = (NB - RING) // RING
            with pool.Fori(1, turns) as j:
                for s in range(RING):
                    edge_step1(j * RING + s, s, j)
            for i in range(turns * RING, NB):
                edge_step1(i, i % RING, turns)

            def inverse_std(c, added, value, ready):
                nc.gpsimd.tensor_scalar(n_var[:, c, :], n_mv[:, c, :, 1], EPS, None, ALU.add).then_inc(added, 1)
                pool.wait_ge(added, value)
                pool.sem_inc(passed, 1)
                nc.gpsimd.tensor_tensor(n_rstd[:, c, :], n_var[:, c, :], minus_half[:, :], ALU.pow).then_inc(ready, 1)

            def gru_step(g, s, j):
                c, b = (s - 1) % 2, (s - 1) % RING
                if in_range(g - 1, NG):
                    pool.wait_ge(z_ready, g)
                    pool.sem_inc(passed, 1)
                    pool.wait_ge(hf_ready, used(g - 2))
                    pool.sem_inc(passed, 1)
                    nc.gpsimd.tensor_tensor(zh_sb[:, c, :], z_sb[:, c, :], xt1[:, b, :], ALU.mult)\
                        .then_inc(zh_ready, 1)
                    pool.wait_ge(zh_ready, g)
                    pool.sem_inc(passed, 1)
                    pool.wait_ge(zn_ready, g)
                    pool.sem_inc(passed, 1)
                    pool.wait_ge(back_done, used(g - 2))
                    pool.sem_inc(passed, 1)
                    nc.gpsimd.tensor_tensor(hf_sb[:, c, :], zh_sb[:, c, :], zn_sb[:, c, :], ALU.subtract)\
                        .then_inc(hf_ready, 1)
                if in_range(g - 2, NG):
                    pool.wait_ge(ymv_ready, g - 1)
                    pool.sem_inc(passed, 1)
                    inverse_std(s % 2, yeps_done, g - 1, yrstd_ready)
            steps(pool, NG, gru_step, lag=2)

        @block.tensor
        def _(pe):
            def mm(to, left, right, start=True, stop=True):
                return nc.tensor.matmul(to, left, right, start=start, stop=stop)

            pe.wait_ge(pool_set, 3)
            pe.wait_ge(rows_ready, 1)
            for n in range(4):
                for c in range(2):
                    at = (n // 2) * W + (n % 2) * TILES + c * HALF
                    last = nc.tensor.transpose(turned_ps[:, at:at + HALF], rows_f[0:HALF, n, c, :],
                                               ident[0:HALF, 0:HALF])
            last.then_inc(setup_turned, 1)
            pe.wait_ge(weights_in, WEIGHT_LOADS * DMA)
            nc.tensor.transpose(bank[2][:, 0:P], wmsg_raw[:, :], ident[:, :])
            for b in range(3):
                nc.tensor.transpose(bank[0][:, b * P:(b + 1) * P], wih_raw[:, b, :], ident[:, :])
            for b in range(3):
                last = nc.tensor.transpose(bank[1][:, b * P:(b + 1) * P], whh_raw[:, b, :], ident[:, :])
            last.then_inc(setup_turned, 1)
            pe.wait_ge(weights_ready, 1)
            pe.wait_ge(index_ready, 1)

            def turn(ps, rows):
                for k in range(K):
                    last = nc.tensor.transpose(ps[:, k * P:(k + 1) * P], rows[:, k * P:(k + 1) * P], ident[:, :])
                return last

            def equal_sums(ps, values, c):
                for k in reversed(range(K)):
                    n = (k + 1) * P
                    last = mm(ps[:, 0:n], values(k), equal[:, c, eq_at(k):eq_at(k) + n],
                              start=(k == K - 1), stop=(k == 0))
                return last

            h1t_ps, h1_ps, h1n_ps, h2t_ps, h2_ps, sumt_ps = bank
            sum_ps = h1t_ps

            def edge_step(i, s, j):
                c = s % 2
                if in_range(i, NB):
                    pe.wait_ge(gathered[s], (j + 1) * 2 * K * DMA)
                    pe.wait_ge(xt_ready, used(i))
                    for k in range(2 * K):
                        last = nc.tensor.transpose(turned_ps[:, k * P:(k + 1) * P], xg[:, s, k, :], ident[:, :])
                    last.then_inc(xg_turned, 1)
                if in_range(i - 1, NB):
                    pe.wait_ge(h1n_ready, used(i))
                    pe.wait_ge(y1_ready, used(i - 1))
                    turn(h1n_ps, h1n[:, 1 - c]).then_inc(h1n_turned, 1)
                if in_range(i, NB):
                    pe.wait_ge(xt_ready, i + 1)
                    pe.wait_ge(total_ready, used(i - 3))
                    mm(h1t_ps[:, :], w1_sb[:, 0, :], xt[:, c, 0:W], stop=False)
                    mm(h1t_ps[:, :], w1_sb[:, 1, :], xt[:, c, W:], start=False).then_inc(h1_done, 1)
                if in_range(i - 1, NB):
                    pe.wait_ge(act1_ready, i)
                    pe.wait_ge(h2t_ready, used(i - 1))
                    mm(h2t_ps[:, :], w2_sb[:, :], act1[:, 1 - c, :]).then_inc(h2_done, 1)
                if in_range(i, NB):
                    pe.wait_ge(h1t_ready, i + 1)
                    pe.wait_ge(h1n_ready, used(i))
                    turn(h1_ps, h1t_sb).then_inc(h1_back, 1)
                if in_range(i - 1, NB):
                    pe.wait_ge(h2t_ready, i)
                    pe.wait_ge(h2n_ready, used(i - 1))
                    turn(h2_ps, h2t_sb).then_inc(h2_back, 1)
                if in_range(i - 2, NB):
                    pe.wait_ge(hout_ready, i - 1)
                    pe.wait_ge(equal_made, i - 1)
                    pe.wait_ge(sumt_ready, used(i - 2))
                    equal_sums(sumt_ps, lambda k: hout[:, c, k * P:(k + 1) * P], c).then_inc(sums_done, 1)
                if in_range(i - 2, NB):
                    pe.wait_ge(sumt_ready, i - 1)
                    pe.wait_ge(h1t_ready, i + 1 if in_range(i, NB) else NB)
                    turn(sum_ps, sumt_sb).then_inc(sums_back, 1)
            steps(pe, NB, edge_step, lag=2)

            msgt_ps, msg_ps = bank[4], bank[5]

            def edge_step1(i, s, j):
                c = s % 2
                if in_range(i - 1, NB):
                    pe.wait_ge(at_ready, i)
                    pe.wait_ge(msgt_ready, used(i - 1))
                    mm(msgt_ps[:, :], wmsg_t[:, :], at_sb[:, 1 - c, :], stop=False)
                    mm(msgt_ps[:, :], embb[:, :], ct_sb[:, 1 - c, :], start=False).then_inc(msg_done, 1)
                if in_range(i, NB):
                    pe.wait_ge(gathered1[s], (j + 1) * K * DMA)
                    pe.wait_ge(equal1_made, i + 1)
                    pe.wait_ge(at_ready, used(i - 1))
                    equal_sums(bank[c], lambda k: xg[:, s, k, :], c)
                    equal_sums(bank[2 + c][0:T_TYPES], lambda k: onehot[:, c, k, :], c).then_inc(edge_sums, 1)
                if in_range(i - 1, NB):
                    pe.wait_ge(msgt_ready, i)
                    pe.wait_ge(msg_ready, used(i - 1))
                    turn(msg_ps, msgt_sb).then_inc(msg_back, 1)
            steps(pe, NB, edge_step1, lag=1)

            r_ps, hn_ps, z_ps, in_ps, back_ps = bank[0], bank[1], bank[2], bank[3], bank[5]

            def gru_step(g, s, j):
                c = s % 2
                if in_range(g, NG):
                    pe.wait_ge(s_in[s], (j + 1) * DMA)
                    pe.wait_ge(mt_ready, used(g))
                    for k in range(K):
                        nc.tensor.transpose(turned_ps[:, k * P:(k + 1) * P], ng_s[:, s, k * P:(k + 1) * P],
                                            ident[:, :])
                    pe.wait_ge(x1_in[s], (j + 1) * DMA)
                    pe.wait_ge(xt1_ready, used(g))
                    for k in range(K):
                        last = nc.tensor.transpose(turned_ps[:, W + k * P:W + (k + 1) * P],
                                                   ng_x[:, s, k * P:(k + 1) * P], ident[:, :])
                    last.then_inc(g_turned, 1)
                if in_range(g - 1, NG):
                    m, h = mt[:, 1 - c, :], xt1[:, (s - 1) % RING, :]
                    pe.wait_ge(mt_ready, used(g))
                    pe.wait_ge(xt1_ready, used(g))
                    pe.wait_ge(r_ready, used(g - 1))
                    mm(r_ps[:, :], wih_t[:, 0:P], m, stop=False)
                    mm(r_ps[:, :], whh_t[:, 0:P], h, start=False).then_inc(r_done, 1)
                    pe.wait_ge(rh_ready, used(g - 1))
                    mm(hn_ps[:, :], whh_t[:, 2 * P:], h).then_inc(hn_done, 1)
                    pe.wait_ge(pre_ready, used(g - 1))
                    mm(in_ps[:, :], wih_t[:, 2 * P:], m).then_inc(in_done, 1)
                    pe.wait_ge(z_ready, used(g - 1))
                    mm(z_ps[:, :], wih_t[:, P:2 * P], m, stop=False)
                    mm(z_ps[:, :], whh_t[:, P:2 * P], h, start=False).then_inc(z_done, 1)
                if in_range(g - 2, NG):
                    pe.wait_ge(hf_ready, g - 1)
                    pe.wait_ge(y_ready, used(g - 2))
                    for k in range(K):
                        last = nc.tensor.transpose(back_ps[:, k * P:(k + 1) * P],
                                                   hf_sb[:, c, k * P:(k + 1) * P], ident[:, :])
                    last.then_inc(back_done, 1)
            steps(pe, NG, gru_step, lag=2)

        @block.scalar
        def _(act):
            h1t_ps, h1_ps, h1n_ps, h2t_ps, h2_ps, sumt_ps = bank
            sum_ps = h1t_ps
            act.wait_ge(cols_made, 1)
            for z in range(ZCHUNKS):
                act.dma_start(zero_chunk(agg, z), zeros[:, :]).then_inc(agg_zeroed, DMA)
            act.wait_ge(weights_ready, 1)

            def normalise_rows(to, ps, scales, biases, ready):
                for k in range(K):
                    last = nc.scalar.activation(to[:, k * P:(k + 1) * P], ps[:, k * P:(k + 1) * P], ACT.Identity,
                                                bias=biases[:, k:k + 1], scale=scales[:, k:k + 1])
                last.then_inc(ready, 1)

            def edge_step(i, s, j):
                c = s % 2
                if in_range(i, NB):
                    act.wait_ge(xg_turned, i + 1)
                    act.wait_ge(h1_done, used(i - 1))
                    nc.scalar.activation(xt[:, c, 0:W], turned_ps[:, 0:W], ACT.Copy)
                    nc.scalar.activation(xt[:, c, W:], turned_ps[:, W:], ACT.Copy).then_inc(xt_ready, 1)
                if in_range(i - 1, NB):
                    act.wait_ge(h1n_turned, i)
                    act.wait_ge(act1_ready, used(i - 2))
                    nc.scalar.activation(y1[:, 1 - c, :], h1n_ps[:, :], ACT.Identity, bias=be1_col[:, 0:1],
                                         scale=g1_col[:, 0:1]).then_inc(y1_ready, 1)
                if in_range(i - 2, NB):
                    act.wait_ge(shift2_ready, i - 1)
                    act.wait_ge(h2g_ready, used(i - 2))
                    normalise_rows(h2n, h2_ps, rstd[:, 1], shift[:, 1], h2n_ready)
                if in_range(i, NB):
                    act.wait_ge(h1_done, i + 1)
                    act.wait_ge(h1_back, used(i))
                    nc.scalar.activation(h1t_sb[:, :], h1t_ps[:, :], ACT.Identity, bias=b1_col[:, 0:1])\
                        .then_inc(h1t_ready, 1)
                if in_range(i - 1, NB):
                    act.wait_ge(h2_done, i)
                    act.wait_ge(h2_back, used(i - 1))
                    nc.scalar.activation(h2t_sb[:, :], h2t_ps[:, :], ACT.Identity, bias=b2_col[:, 0:1])\
                        .then_inc(h2t_ready, 1)
                if in_range(i, NB):
                    act.wait_ge(mv1_ready, i + 1)
                    nc.scalar.activation(std[:, 0, :], mv[:, 0, :, 1], ACT.Sqrt, bias=eps_col[:, 0:1])\
                        .then_inc(std1_ready, 1)
                if in_range(i - 2, NB):
                    act.wait_ge(sums_done, i - 1)
                    act.wait_ge(sums_back, used(i - 2))
                    nc.scalar.activation(sumt_sb[:, :], sumt_ps[:, :], ACT.Copy).then_inc(sumt_ready, 1)
                if in_range(i, NB):
                    act.wait_ge(shift1_ready, i + 1)
                    act.wait_ge(h1n_turned, used(i - 1))
                    normalise_rows(h1n[:, c], h1_ps, rstd[:, 0], shift[:, 0], h1n_ready)
                if in_range(i - 2, NB):
                    act.wait_ge(sums_back, i - 1)
                    act.wait_ge(scattered, used((i - 3) * K * DMA))
                    nc.scalar.activation(total[:, (s - 2) % RING, :], sum_ps[:, :], ACT.Copy)\
                        .then_inc(total_ready, 1)
                if in_range(i - 1, NB):
                    act.wait_ge(mv2_ready, i)
                    nc.scalar.activation(std[:, 1, :], mv[:, 1, :, 1], ACT.Sqrt, bias=eps_col[:, 0:1])\
                        .then_inc(std2_ready, 1)
            steps(act, NB, edge_step, lag=2)

            def node_step(g, s, j):
                if in_range(g, NG):
                    act.wait_ge(nmv_ready, g + 1)
                    nc.scalar.activation(n_var[:, s % 2, :], n_mv[:, s % 2, :, 1], ACT.Sqrt, bias=eps_col[:, 0:1])\
                        .then_inc(nstd_ready, 1)
                if in_range(g - 1, NG):
                    b = (s - 1) % RING
                    act.wait_ge(nshift_ready, g)
                    if not isinstance(g, int) or g > RING:
                        act.wait_ge(x1_out[b], (j if s else j - 1) * DMA)
                    normalise_rows(ng_o[:, b], ng_s[:, b], n_rstd[:, (s - 1) % 2], n_shift[:, (s - 1) % 2], x1_ready)
                    act.wait_ge(x1_ready, g)
                    if isinstance(g, int) and g == NG:
                        act.wait_ge(x1_out[(s - 2) % RING], ((g - 2) // RING + 1) * DMA)
                    act.dma_start(group(x1, g - 1), ng_o[:, b, :]).then_inc(x1_out[b], DMA)
            steps(act, NG, node_step, lag=1)

            msgt_ps, msg_ps = bank[4], bank[5]

            def edge_step1(i, s, j):
                c = s % 2
                if in_range(i - 1, NB):
                    act.wait_ge(msg_done, i)
                    act.wait_ge(msg_back, used(i - 1))
                    nc.scalar.activation(msgt_sb[:, :], msgt_ps[:, :], ACT.Copy).then_inc(msgt_ready, 1)
                if in_range(i, NB):
                    act.wait_ge(edge_sums, i + 1)
                    act.wait_ge(msg_done, used(i - 1))
                    nc.scalar.activation(at_sb[:, c, :], bank[c][:, :], ACT.Copy)
                    nc.scalar.activation(ct_sb[:, c, :], bank[2 + c][0:T_TYPES, :], ACT.Copy).then_inc(at_ready, 1)
                if in_range(i - 1, NB):
                    act.wait_ge(msg_back, i)
                    act.wait_ge(scattered1, used((i - 3) * K * DMA))
                    nc.scalar.activation(total[:, (s - 1) % RING, :], msg_ps[:, :], ACT.Copy)\
                        .then_inc(msg_ready, 1)
            steps(act, NB, edge_step1, lag=1)

            r_ps, z_ps = bank[0], bank[2]

            def gru_step(g, s, j):
                c = s % 2
                if in_range(g, NG):
                    act.wait_ge(g_turned, g + 1)
                    act.wait_ge(in_done, used(g - 1))
                    act.wait_ge(z_done, used(g - 1))
                    nc.scalar.activation(mt[:, c, :], turned_ps[:, 0:W], ACT.Copy).then_inc(mt_ready, 1)
                    act.wait_ge(zh_ready, used(g - RING + 1))
                    nc.scalar.activation(xt1[:, s, :], turned_ps[:, W:], ACT.Copy).then_inc(xt1_ready, 1)
                if in_range(g - 1, NG):
                    act.wait_ge(r_done, g)
                    act.wait_ge(rh_ready, used(g - 2))
                    nc.scalar.activation(r_sb[:, 1 - c, :], r_ps[:, :], ACT.Sigmoid, bias=brz_col[:, 0:1])\
                        .then_inc(r_ready, 1)
                    act.wait_ge(z_done, g)
                    act.wait_ge(zh_ready, used(g - 2))
                    act.wait_ge(zn_ready, used(g - 2))
                    nc.scalar.activation(z_sb[:, 1 - c, :], z_ps[:, :], ACT.Sigmoid, bias=brz_col[:, 1:2])\
                        .then_inc(z_ready, 1)
                    act.wait_ge(pre_ready, g)
                    act.wait_ge(zn_ready, used(g - 2))
                    nc.scalar.activation(n_sb[:, 1 - c, :], pre_n[:, 1 - c, :], ACT.Tanh, bias=bih_col[:, 2:3])\
                        .then_inc(n_ready, 1)
                if in_range(g - 4, NG):
                    act.wait_ge(o_ready, g - 3)
                    if isinstance(g, int) and g - 4 == NG - 1:
                        act.wait_ge(out_done[(s - 5) % RING], ((g - 5) // RING + 1) * DMA)
                    act.dma_start(group(out, g - 4), ng_o[:, s, :]).then_inc(out_done[s], DMA)
            steps(act, NG, gru_step, lag=4)
            for s in range(RING):
                act.wait_ge(out_done[s], ((NG - 1 - s) // RING + 1) * DMA)

        @block.vector
        def _(dve):
            nc.vector.memset(zeros[:, :], 0.0)
            nc.vector.memset(eps_col[:, :], EPS).then_inc(cols_made, 1)
            dve.wait_ge(edges_in, EDGE_LOADS * DMA)
            nc.vector.tensor_copy(rows_f[0:HALF, 0:3], rows_i[0:HALF]).then_inc(rows_ready, 1)
            dve.wait_ge(setup_turned, 1)
            dve.wait_ge(pool_set, 7)

            def turned(n):
                at = (n // 2) * W + (n % 2) * TILES
                return turned_ps[:, at:at + TILES].rearrange("p (b k) -> p b k", k=K)

            nc.vector.tensor_copy(gather_idx[:, :, 0:K], turned(0))
            nc.vector.tensor_scalar(gather_idx[:, :, K:], turned(1), float(N - 1), None, ALU.min)
            nc.vector.tensor_copy(dst_col[:, :, :], turned(1)).then_inc(cols_made, 1)
            nc.vector.tensor_scalar(type_col[:, :, :], turned(2), 0.0, float(T_TYPES - 1), ALU.max, ALU.min)
            nc.vector.tensor_copy(w_col[:, :, :], turned(3))
            dve.wait_ge(cols_made, 2)
            nc.vector.tensor_tensor(to_spill[:, :, :], spill_row[:, :, :], dst_col[:, :, :], ALU.subtract)\
                .then_inc(index_ready, 1)
            dve.wait_ge(setup_turned, 2)
            nc.vector.tensor_copy(wmsg_t[:, :], bank[2][:, 0:P])
            nc.vector.tensor_copy(wih_t[:, :], bank[0][:, 0:3 * P])
            nc.vector.tensor_copy(whh_t[:, :], bank[1][:, 0:3 * P])
            nc.vector.tensor_tensor(brz_col[:, :], bih_col[:, 0:2], bhh_col[:, 0:2], ALU.add)
            nc.vector.tensor_tensor(embb[:, :], emb_sb[:, :], bmsg_all[:, :], ALU.add).then_inc(weights_ready, 1)
            dve.wait_ge(index_ready, 1)

            h1_ps, h2_ps = bank[1], bank[4]

            def equalities(i, c, weighted, made):
                for k in range(K):
                    n = (k + 1) * P
                    last = nc.vector.tensor_scalar(
                        equal[:, c, eq_at(k):eq_at(k) + n], dst_row[:, c, 0:n], dst_col[:, i, k:k + 1],
                        w_col[:, i, k:k + 1] if weighted else None, ALU.is_equal,
                        ALU.mult if weighted else ALU.bypass)
                last.then_inc(made, 1)

            def row_stats(ps, to_stats, to_mv, done, value, ready):
                for k in range(K):
                    last = nc.vector.bn_stats(to_stats[:, k, :], ps[:, k * P:(k + 1) * P])
                last.then_inc(done, 1)
                dve.wait_ge(done, value)
                dve.sem_inc(passed, 1)
                for k in range(K):
                    last = nc.vector.bn_aggr(to_mv[:, k, :], to_stats[:, k, :])
                last.then_inc(ready, 1)

            def normalise(to, ps, means, scales, ready):
                for k in range(K):
                    last = nc.vector.tensor_scalar(to[:, k * P:(k + 1) * P], ps[:, k * P:(k + 1) * P],
                                                   means[:, k, 0:1], scales[:, k:k + 1], ALU.subtract, ALU.mult)
                last.then_inc(ready, 1)

            def every_tile(row):
                return row[:, None, :].to_broadcast([P, K, P])

            def tiles(a):
                return a.rearrange("p (k f) -> p k f", k=K)

            def scales(n, c, got_std, value, recip, ready):
                dve.wait_ge(got_std, value)
                nc.vector.reciprocal(rstd[:, n, :], std[:, n, :]).then_inc(recip, 1)
                dve.wait_ge(recip, value)
                nc.vector.scalar_tensor_tensor(out=shift[:, n, :], in0=mv[:, n, :, 0], scalar=-1.0,
                                               in1=rstd[:, n, :], op0=ALU.mult, op1=ALU.mult).then_inc(ready, 1)

            def edge_step(i, s, j):
                c = s % 2
                b, e = i - 1, 1 - c
                if in_range(i - 1, NB):
                    dve.wait_ge(y1_ready, i)
                    dve.wait_ge(h2_done, used(i - 2))
                    nc.vector.scalar_tensor_tensor(out=act1[:, 1 - c, :], in0=y1[:, 1 - c, :], scalar=SLOPE,
                                                   in1=y1[:, 1 - c, :], op0=ALU.mult, op1=ALU.max)\
                        .then_inc(act1_ready, 1)
                if in_range(i - 2, NB):
                    dve.wait_ge(h2n_ready, i - 1)
                    nc.vector.tensor_tensor(tiles(h2g[:, :]), tiles(h2n[:, :]), every_tile(g2_all), ALU.mult)\
                        .then_inc(h2g_ready, 1)
                    dve.wait_ge(h2g_ready, i - 1)
                    nc.vector.tensor_tensor(tiles(h2b[:, :]), tiles(h2g[:, :]), every_tile(be2_all), ALU.add)\
                        .then_inc(h2b_ready, 1)
                    dve.wait_ge(h2b_ready, i - 1)
                    dve.wait_ge(sums_done, used(i - 3))
                    nc.vector.scalar_tensor_tensor(out=hout[:, c, :], in0=h2b[:, :], scalar=SLOPE,
                                                   in1=h2b[:, :], op0=ALU.mult, op1=ALU.max)\
                        .then_inc(hout_ready, 1)
                if in_range(i, NB):
                    dve.wait_ge(h1_back, i + 1)
                    dve.wait_ge(h1n_ready, used(i))
                    row_stats(h1_ps, stats[:, 0], mv[:, 0], st1_done, i + 1, mv1_ready)
                if in_range(i - 1, NB):
                    dve.wait_ge(dstrow_in[e], (2 * j + (s - 1) // 2 + 1) * DMA)
                    for k in range(K):
                        n = (k + 1) * P
                        last = nc.vector.scalar_tensor_tensor(
                            out=junk[:, k, 0:n], in0=dst_row[:, e, 0:n], scalar=dst_col[:, b, k:k + 1],
                            in1=before[:, W - n:], op0=ALU.is_equal, op1=ALU.mult, accum_out=dups[:, e, k:k + 1])
                    last.then_inc(dup_done, 1)
                if in_range(i, NB):
                    scales(0, c, std1_ready, i + 1, rstd1_ready, shift1_ready)
                if in_range(i - 1, NB):
                    dve.wait_ge(dup_done, i)
                    nc.vector.scalar_tensor_tensor(out=moved[:, e, :], in0=dups[:, e, :], scalar=0.0,
                                                   in1=to_spill[:, b, :], op0=ALU.is_gt, op1=ALU.mult)\
                        .then_inc(moved_done, 1)
                    dve.wait_ge(sums_done, used(i - 2))
                    equalities(b, e, True, equal_made)
                    dve.wait_ge(moved_done, i)
                    nc.vector.tensor_tensor(scatter_idx[:, b, :], moved[:, e, :], dst_col[:, b, :], ALU.add)\
                        .then_inc(sidx_made, 1)
                    dve.wait_ge(h2_back, i)
                    row_stats(h2_ps, stats[:, 1], mv[:, 1], st2_done, i, mv2_ready)
                    scales(1, e, std2_ready, i, rstd2_ready, shift2_ready)
            steps(dve, NB, edge_step, lag=2)

            def node_step(g, s, j):
                if in_range(g, NG):
                    dve.wait_ge(res_ready, g + 1)
                    row_stats(ng_s[:, s], n_stats[:, s % 2], n_mv[:, s % 2], nst_done, g + 1, nmv_ready)
                if in_range(g, NG):
                    dve.wait_ge(nstd_ready, g + 1)
                    dve.wait_ge(x1_ready, used(g - 1))
                    nc.vector.reciprocal(n_rstd[:, s % 2, :], n_var[:, s % 2, :]).then_inc(nrstd_ready, 1)
                    dve.wait_ge(nrstd_ready, g + 1)
                    nc.vector.scalar_tensor_tensor(out=n_shift[:, s % 2, :], in0=n_mv[:, s % 2, :, 0], scalar=-1.0,
                                                   in1=n_rstd[:, s % 2, :], op0=ALU.mult, op1=ALU.mult)\
                        .then_inc(nshift_ready, 1)
            steps(dve, NG, node_step)

            def edge_step1(i, s, j):
                c = s % 2
                dve.wait_ge(dstrow1_in[c], (2 * j + s // 2 + 1) * DMA)
                dve.wait_ge(edge_sums, used(i - 1))
                nc.vector.tensor_tensor(
                    onehot[:, c], type_col[:, i, :].rearrange("p (k a) -> p k a", a=1).to_broadcast([P, K, T_TYPES]),
                    type_no[:, None, :].to_broadcast([P, K, T_TYPES]), ALU.is_equal)
                equalities(i, c, False, equal1_made)
            steps(dve, NB, edge_step1)

            hn_ps, in_ps, back_ps = bank[1], bank[3], bank[5]

            def gru_step(g, s, j):
                c = s % 2
                if in_range(g - 2, NG):
                    dve.wait_ge(n_ready, g - 1)
                    dve.wait_ge(z_ready, g - 1)
                    dve.wait_ge(hf_ready, used(g - 3))
                    nc.vector.scalar_tensor_tensor(out=zn_sb[:, c, :], in0=z_sb[:, c, :], scalar=-1.0,
                                                   in1=n_sb[:, c, :], op0=ALU.add, op1=ALU.mult)\
                        .then_inc(zn_ready, 1)
                if in_range(g - 1, NG):
                    dve.wait_ge(hn_done, g)
                    dve.wait_ge(r_ready, g)
                    dve.wait_ge(pre_ready, used(g - 2))
                    nc.vector.scalar_tensor_tensor(out=rh_sb[:, 1 - c, :], in0=hn_ps[:, :], scalar=bhh_col[:, 2:3],
                                                   in1=r_sb[:, 1 - c, :], op0=ALU.add, op1=ALU.mult)\
                        .then_inc(rh_ready, 1)
                    dve.wait_ge(rh_ready, g)
                    dve.wait_ge(in_done, g)
                    dve.wait_ge(n_ready, used(g - 2))
                    nc.vector.tensor_tensor(pre_n[:, 1 - c, :], rh_sb[:, 1 - c, :], in_ps[:, :], ALU.add)\
                        .then_inc(pre_ready, 1)
                if in_range(g - 3, NG):
                    dve.wait_ge(yrstd_ready, g - 2)
                    if not isinstance(g, int) or g - 3 >= RING:
                        dve.wait_ge(out_done[(s - 3) % RING], (j if s >= 3 else j - 1) * DMA)
                    normalise(ng_o[:, (s - 3) % RING], y_sb[:, 1 - c], n_mv[:, 1 - c], n_rstd[:, 1 - c], o_ready)
                if in_range(g - 2, NG):
                    dve.wait_ge(back_done, g - 1)
                    nc.vector.tensor_tensor(y_sb[:, c, :], back_ps[:, :], ng_x[:, (s - 2) % RING, :], ALU.add)\
                        .then_inc(y_ready, 1)
                    dve.wait_ge(y_ready, g - 1)
                    row_stats(y_sb[:, c], n_stats[:, c], n_mv[:, c], yst_done, g - 1, ymv_ready)
            steps(dve, NG, gru_step, lag=3)


EDGE_LOADS = 12
WEIGHT_LOADS = 15

_INS = ['x', 'src', 'dst', 'edge_type_9', 'edge_weight', 'L0_gnn_w1', 'L0_gnn_b1', 'L0_gnn_g1', 'L0_gnn_be1',
        'L0_gnn_w2', 'L0_gnn_b2', 'L0_gnn_g2', 'L0_gnn_be2', 'L1_gnn_W_msg', 'L1_gnn_b_msg', 'L1_gnn_edge_embed',
        'L1_gnn_W_ih', 'L1_gnn_W_hh', 'L1_gnn_b_ih', 'L1_gnn_b_hh']


def kernel(**inputs):
    import numpy as _np
    import concourse.bacc as _bacc
    from concourse import mybir as _mybir
    from concourse.bass_utils import run_bass_kernel_spmd as _run

    nc = _bacc.Bacc("TRN2", target_bir_lowering=False, num_devices=1)
    arrays, args = {}, []
    for name in _INS:
        a = _np.ascontiguousarray(inputs[name])
        arrays[f"in_{name}"] = a
        args.append(nc.dram_tensor(f"in_{name}", a.shape, _mybir.dt.from_np(a.dtype), kind="ExternalInput").ap())
    shape = inputs['x'].shape
    args.append(nc.dram_tensor("out_0", shape, _mybir.dt.float32, kind="ExternalOutput").ap())
    gnn_kernel(nc, *args)
    r = _run(nc, [arrays], core_ids=[0])
    return r.results[0]["out_0"]
```

```python
from contextlib import ExitStack

import concourse.bass as bass
from concourse import mybir

F32 = mybir.dt.float32
I32 = mybir.dt.int32
F32R = mybir.dt.float32r
ALU = mybir.AluOpType
ACT = mybir.ActivationFunctionType

P = 128
K = 4
W = K * P
RING = 4
DEEP = 2 * RING
EPS = 1e-5
SLOPE = 0.2
DMA = 16


def gnn_kernel(nc, x, src, dst, edge_type, edge_weight, w1, b1, g1, be1, w2, b2, g2, be2,
               W_msg, b_msg, edge_embed, W_ih, W_hh, b_ih, b_hh, out):
    N, H = x.shape
    E = src.shape[0]
    T_TYPES = edge_embed.shape[0]
    NB = -(-E // W)
    TILES = NB * K
    HALF = TILES // 2
    NG = N // W + 1
    NG0 = N // (2 * W) + 1
    ROWS = -(-(N + W) // (16 * P)) * 16 * P
    ZCOLS = 2560
    ZCHUNKS = ROWS * H // (P * ZCOLS)
    CCHUNKS = 20
    COPY_AFTER = [0, 11, 4, 3]
    assert N % W and N % (2 * W) and (ROWS - N) * H % ZCOLS == 0 and N * H % (CCHUNKS * P) == 0 and 2 + sum(COPY_AFTER) == CCHUNKS
    assert ZCHUNKS == 2 * (NB // RING) - RING
    assert H == P and TILES == 2 * HALF and HALF <= P and ZCHUNKS * ZCOLS * P == ROWS * H
    whole_rows = E // P - HALF
    rest = E - (E // P) * P
    assert rest and whole_rows == HALF - 1
    PAD_TARGET = N + (K - 1) * P

    def eq_at(k):
        return P * k * (k + 1) // 2

    agg = nc.dram_tensor("agg", [ROWS, H], F32, kind="Internal").ap()
    msum = nc.dram_tensor("msum", [ROWS, H], F32, kind="Internal").ap()
    x1 = nc.dram_tensor("x1", [N, H], F32, kind="Internal").ap()
    dpad = nc.dram_tensor("dpad", [NB, W], I32, kind="Internal").ap()

    def groups(t, w):
        full = N // w * w
        return (t[0:full, :].rearrange("(g p j) f -> g p (j f)", p=P, j=w // P),
                t[N - w:N, :].rearrange("(p j) f -> p (j f)", p=P))

    def zero_chunk(t, z):
        return t.rearrange("(p r) f -> p (r f)", p=P).rearrange("p (z c) -> z p c", c=ZCOLS)[z]

    def copy_chunk(t, z):
        return t[0:N, :].rearrange("n f -> (n f)").rearrange("(c p e) -> c p e", c=CCHUNKS, p=P)[z]

    def group(t, g, w=W):
        whole, last = groups(t, w)
        return last if isinstance(g, int) and g == N // w else whole[g]

    ctx = ExitStack()
    with ctx:
        def sb(name, shape, dt=F32):
            return ctx.enter_context(nc.sbuf_tensor(name, shape, dt))

        def sem(name):
            return ctx.enter_context(nc.semaphore(name))

        def sem_ring(name):
            return [sem(f"{name}{s}") for s in range(RING)]

        bank = [ctx.enter_context(nc.psum_tensor(f"bank{b}", [P, W], F32)) for b in range(6)]
        turned_ps = ctx.enter_context(nc.psum_tensor("turned_ps", [P, 2 * W], F32))

        ident = sb("ident", [P, P])
        before = sb("before", [P, W])
        zeros = sb("zeros", [P, ZCOLS])
        eps_col = sb("eps_col", [P, 1])
        w1_sb = sb("w1_sb", [P, 2, P])
        w2_sb = sb("w2_sb", [P, P])
        b1_col = sb("b1_col", [P, 1])
        b2_col = sb("b2_col", [P, 1])
        g1_col = sb("g1_col", [P, 1])
        be1_col = sb("be1_col", [P, 1])
        g2_all = sb("g2_all", [P, P])
        be2_all = sb("be2_all", [P, P])
        wmsg_raw = sb("wmsg_raw", [P, P])
        wih_raw = sb("wih_raw", [P, 3, P])
        whh_raw = sb("whh_raw", [P, 3, P])
        wmsg_t = sb("wmsg_t", [P, P])
        wih_t = sb("wih_t", [P, 2, 3 * P], F32R)
        whh_t = sb("whh_t", [P, 2, 3 * P], F32R)
        bih_col = sb("bih_col", [P, 3])
        bhh_col = sb("bhh_col", [P, 3])
        brz_col = sb("brz_col", [P, 2])
        emb_sb = sb("emb_sb", [T_TYPES, P])
        bmsg_all = sb("bmsg_all", [T_TYPES, P])
        embb = sb("embb", [T_TYPES, P])
        type_no = sb("type_no", [P, T_TYPES])
        rows_i = sb("rows_i", [P, 3, 2, P], I32)
        rows_f = sb("rows_f", [P, 4, 2, P])
        gather_idx = sb("gather_idx", [P, NB + RING, 2 * K], I32)
        scatter_idx = sb("scatter_idx", [P, NB, K], I32)
        dst_col = sb("dst_col", [P, NB, K])
        spill_row = sb("spill_row", [P, NB, K], I32)
        to_spill = sb("to_spill", [P, NB, K])
        type_col = sb("type_col", [P, NB, K])
        w_col = sb("w_col", [P, NB, K])
        gidx_slot = sb("gidx_slot", [P, RING, 2 * K], I32)
        sidx_slot = sb("sidx_slot", [P, DEEP, K], I32)
        xg = sb("xg", [P, RING, 2 * K, P])
        dst_row = sb("dst_row", [P, 2, W], I32)
        equal = sb("equal", [P, 2, eq_at(K)])
        equal1 = sb("equal1", [P, 2, eq_at(K)], F32R)
        junk = sb("junk", [P, K, W])
        dups = sb("dups", [P, 2, K])
        moved = sb("moved", [P, 2, K])
        xt = sb("xt", [P, 2, 2 * W])
        h1n = sb("h1n", [P, 2, W])
        y1 = sb("y1", [P, 2, W])
        act1 = sb("act1", [P, 2, W])
        h1t_sb = sb("h1t_sb", [P, W])
        h2t_sb = sb("h2t_sb", [P, W])
        sumt_sb = sb("sumt_sb", [P, W])
        msgt_sb = sb("msgt_sb", [P, W])
        h2n = sb("h2n", [P, W])
        h2g = sb("h2g", [P, W])
        h2b = sb("h2b", [P, W])
        hout = sb("hout", [P, 2, W])
        total = sb("total", [P, RING, W])
        stats = sb("stats", [P, 2, K, 6])
        mv = sb("mv", [P, 2, K, 2])
        std = sb("std", [P, 2, K])
        rstd = sb("rstd", [P, 2, K])
        shift = sb("shift", [P, 2, K])
        onehot = sb("onehot", [P, 2, K, T_TYPES], F32R)
        at_sb = sb("at_sb", [P, 2, W])
        ct_sb = sb("ct_sb", [T_TYPES, 2, W])
        node_in = sb("node_in", [P, RING, 2 * W])
        total0 = node_in.rearrange("p s (d w) -> p (s d) w", w=W)
        n_stats = sb("n_stats", [P, 2, 2 * K, 6])
        n_mv = sb("n_mv", [P, 2, 2 * K, 2])
        n_shift = sb("n_shift", [P, 2, 2 * K])
        n_var = sb("n_var", [P, 2, 2 * K])
        minus_half = sb("minus_half", [P, K])
        n_rstd = sb("n_rstd", [P, 2, 2 * K])
        mt = sb("mt", [P, 2, 2, W], F32R)
        xt1 = sb("xt1", [P, RING, W])
        xt1_parts = sb("xt1_parts", [P, 2, 2, W], F32R)
        z_sb = sb("z_sb", [P, 2, W])
        r_sb, rh_sb, zx_sb, yt_sb = y1, h1n, act1, hout
        pre_n = sb("pre_n", [P, 2, W])
        n_sb = sb("n_sb", [P, 2, W])
        zn_sb = sb("zn_sb", [P, 2, W])
        ng_o = sb("ng_o", [P, RING, W])

        pool_set = sem("pool_set")
        pads_set = sem("pads_set")
        edges_in = sem("edges_in")
        weights_in = sem("weights_in")
        rows_ready = sem("rows_ready")
        setup_turned = sem("setup_turned")
        weights_ready = sem("weights_ready")
        high_made = sem("high_made")
        cols_made = sem("cols_made")
        index_ready = sem("index_ready")
        dpad_out = sem("dpad_out")
        spill_zeroed = sem("spill_zeroed")
        agg_set = [sem("agg_set0"), sem("agg_set1")]
        msum_zeroed = sem("msum_zeroed")
        passed = sem("passed")
        gidx_made = sem("gidx_made")
        gathered = sem_ring("gathered")
        dstrow_in = [sem("dstrow_in0"), sem("dstrow_in1")]
        equal_made = sem("equal_made")
        dup_done = sem("dup_done")
        moved_done = sem("moved_done")
        sidx_made = sem("sidx_made")
        xg_turned = sem("xg_turned")
        xt_ready = sem("xt_ready")
        h1_done = sem("h1_done")
        st1_done = sem("st1_done")
        mv1_ready = sem("mv1_ready")
        std1_ready = sem("std1_ready")
        rstd1_ready = sem("rstd1_ready")
        shift1_ready = sem("shift1_ready")
        h1n_ready = sem("h1n_ready")
        h1n_turned = sem("h1n_turned")
        y1_ready = sem("y1_ready")
        act1_ready = sem("act1_ready")
        h1t_ready = sem("h1t_ready")
        h1_back = sem("h1_back")
        h2_done = sem("h2_done")
        h2t_ready = sem("h2t_ready")
        h2_back = sem("h2_back")
        shift2_ready = sem("shift2_ready")
        st2_done = sem("st2_done")
        mv2_ready = sem("mv2_ready")
        std2_ready = sem("std2_ready")
        rstd2_ready = sem("rstd2_ready")
        h2n_ready = sem("h2n_ready")
        h2g_ready = sem("h2g_ready")
        h2b_ready = sem("h2b_ready")
        hout_ready = sem("hout_ready")
        sums_done = sem("sums_done")
        sumt_ready = sem("sumt_ready")
        sums_back = sem("sums_back")
        total_ready = sem("total_ready")
        scattered = sem("scattered")
        agg_in = sem_ring("agg_in") + sem_ring("agg_in_b")
        nst_done = sem("nst_done")
        nmv_ready = sem("nmv_ready")
        nstd_ready = sem("nstd_ready")
        nshift_ready = sem("nshift_ready")
        nrstd_ready = sem("nrstd_ready")
        x1_ready = sem("x1_ready")
        x1_first = sem("x1_first")
        x1_out = sem_ring("x1_out")
        gidx1_made = sem("gidx1_made")
        gathered1 = sem_ring("gathered1")
        dstrow1_in = [sem("dstrow1_in0"), sem("dstrow1_in1")]
        equal1_made = sem("equal1_made")
        edge_sums = sem("edge_sums")
        at_ready = sem("at_ready")
        msg_done = sem("msg_done")
        msgt_ready = sem("msgt_ready")
        msg_back = sem("msg_back")
        msg_ready = sem("msg_ready")
        scattered1 = sem("scattered1")
        s_in = sem_ring("s_in")
        x1_in = sem_ring("x1_in")
        g_turned = sem("g_turned")
        mth_ready = sem("mth_ready")
        xt1_ready = sem("xt1_ready")
        mt_ready = sem("mt_ready")
        xtl_ready = sem("xtl_ready")
        r_done = sem("r_done")
        hn_done = sem("hn_done")
        z_done = sem("z_done")
        in_done = sem("in_done")
        r_ready = sem("r_ready")
        z_ready = sem("z_ready")
        rh_ready = sem("rh_ready")
        pre_ready = sem("pre_ready")
        n_ready = sem("n_ready")
        zn_ready = sem("zn_ready")
        zx_ready = sem("zx_ready")
        yt_ready = sem("yt_ready")
        yshift_ready = sem("yshift_ready")
        back_done = sem("back_done")
        yst_done = sem("yst_done")
        ymv_ready = sem("ymv_ready")
        yeps_done = sem("yeps_done")
        yrstd_ready = sem("yrstd_ready")
        o_ready = sem("o_ready")
        out_done = sem_ring("out_done")

        def steps(eng, count, step, lag=0, body=RING):
            for i in range(body):
                step(i, i, 0)
            turns = count // body
            with eng.Fori(1, turns) as j:
                for s in range(body):
                    step(j * body + s, s, j)
            for i in range(turns * body, count + lag):
                step(i, i % body, i // body)

        def in_range(i, n):
            return not isinstance(i, int) or 0 <= i < n

        def used(count):
            return max(count, 0) if isinstance(count, int) else count

        def as_f32(a):
            return a.bitcast(F32)

        def sums_of(s):
            s %= DEEP
            return node_in[:, s, :] if s < RING else xg[:, s - RING].rearrange("p k f -> p (k f)")

        def result_of(s):
            s %= RING
            return (ng_o, xt1)[s // 2][:, s % 2 * 2:s % 2 * 2 + 2, :].rearrange("p d w -> p (d w)")

        block = ctx.enter_context(nc.Block())

        @block.sync
        def _(sp):
            sp.wait_ge(pads_set, 4)
            sp.sem_inc(passed, 1)
            edge_loads = 0
            whole = HALF * P
            for n, a in enumerate((src, dst, edge_type, edge_weight)):
                to = rows_i[:, n] if n < 3 else rows_f[:, 3]
                sp.dma_start(to[0:HALF, 0, :], a[0:whole].rearrange("(q e) -> q e", e=P)).then_inc(edges_in, DMA)
                sp.dma_start(to[0:whole_rows, 1, :],
                             a[whole:whole + whole_rows * P].rearrange("(q e) -> q e", e=P)).then_inc(edges_in, DMA)
                sp.dma_start(to[whole_rows:HALF, 1, 0:rest],
                             a[E - rest:E].rearrange("(q e) -> q e", q=1)).then_inc(edges_in, DMA)
                edge_loads += 3
            for z in range(2):
                sp.dma_start(copy_chunk(agg, z), copy_chunk(x, z)).then_inc(agg_set[z], DMA)
            with nc.allow_non_contiguous_dma(reason="columns of a few hundred bytes"):
                loads = [
                    (w1_sb[:, :, :], w1.rearrange("(h k) n -> k h n", h=2)), (w2_sb[:, :], w2),
                    (b1_col[:, :], b1.rearrange("(n a) -> n a", a=1)), (b2_col[:, :], b2.rearrange("(n a) -> n a", a=1)),
                    (g1_col[:, :], g1.rearrange("(n a) -> n a", a=1)), (be1_col[:, :], be1.rearrange("(n a) -> n a", a=1)),
                    (g2_all[:, :], g2.partition_broadcast(P)), (be2_all[:, :], be2.partition_broadcast(P)),
                    (wmsg_raw[:, :], W_msg), (wih_raw[:, :, :], W_ih.rearrange("(b p) k -> p b k", b=3)),
                    (whh_raw[:, :, :], W_hh.rearrange("(b p) k -> p b k", b=3)),
                    (bih_col[:, :], b_ih.rearrange("(b p) -> p b", b=3)), (bhh_col[:, :], b_hh.rearrange("(b p) -> p b", b=3)),
                    (emb_sb[:, :], edge_embed), (bmsg_all[:, :], b_msg.partition_broadcast(T_TYPES)),
                ]
                assert len(loads) == WEIGHT_LOADS and edge_loads == EDGE_LOADS
                for to, a in loads:
                    sp.dma_start(to, a).then_inc(weights_in, DMA)
            sp.wait_ge(edges_in, EDGE_LOADS * DMA)
            sp.sem_inc(passed, 1)
            sp.dma_start(dpad.rearrange("b w -> (b w)").rearrange("(c q e) -> q c e", c=2, e=P),
                         rows_i[0:HALF, 1]).then_inc(dpad_out, DMA)
            sp.wait_ge(cols_made, 1)
            sp.sem_inc(passed, 1)
            spill = (ROWS - N) * H // ZCOLS
            sp.dma_start(agg[N:, :].rearrange("n f -> (n f)").rearrange("(q e) -> q e", q=spill), zeros[0:spill, :])\
                .then_inc(spill_zeroed, DMA)
            sp.wait_ge(dpad_out, DMA)
            sp.sem_inc(passed, 1)

            def load_targets(i, s, j):
                sp.wait_ge(sidx_made, used(i - 1))
                sp.sem_inc(passed, 1)
                sp.dma_start(dst_row[:, s % 2, :], dpad[i].partition_broadcast(P))\
                    .then_inc(dstrow_in[s % 2], DMA)

            z = 2
            for i in range(2 * RING):
                load_targets(i, i % RING, i // RING)
                for _ in range(COPY_AFTER[i] if i < len(COPY_AFTER) else 0):
                    sp.wait_ge(agg_set[z % 2], z // 2 * DMA)
                    sp.sem_inc(passed, 1)
                    sp.dma_start(copy_chunk(agg, z), copy_chunk(x, z)).then_inc(agg_set[z % 2], DMA)
                    z += 1
            with sp.Fori(2, NB // RING) as j:
                for s in range(RING):
                    load_targets(j * RING + s, s, j)
                    if s % 2:
                        sp.dma_start(zero_chunk(msum, 2 * j + s // 2 - RING), zeros[:, :]).then_inc(msum_zeroed, DMA)
            for i in range(NB // RING * RING, NB):
                load_targets(i, i % RING, i // RING)

            sp.wait_ge(scattered, NB * K * DMA)
            sp.sem_inc(passed, 1)

            def load_nodes(g, s, j):
                if in_range(g - DEEP, NG0):
                    sp.wait_ge(x1_ready, g - DEEP + 1)
                    sp.sem_inc(passed, 1)
                    sp.wait_ge(x1_first, g - DEEP + 1)
                    sp.sem_inc(passed, 1)
                    if isinstance(g, int) and g - DEEP == NG0 - 1:
                        sp.wait_ge(x1_out[(s - 1) % RING], ((NG0 - 2) // RING + 1) * DMA)
                        sp.sem_inc(passed, 1)
                    sp.dma_start(group(x1, g - DEEP, 2 * W), result_of(s)).then_inc(x1_out[s % RING], DMA)
                if in_range(g, NG0):
                    sp.dma_start(sums_of(s), group(agg, g, 2 * W)).then_inc(agg_in[s], DMA)
            steps(sp, NG0, load_nodes, lag=DEEP, body=DEEP)

            def load_targets1(i, s, _):
                sp.wait_ge(equal1_made, used(i - 1))
                sp.sem_inc(passed, 1)
                sp.dma_start(dst_row[:, s % 2, :], dpad[i].partition_broadcast(P))\
                    .then_inc(dstrow1_in[s % 2], DMA)
            steps(sp, NB, load_targets1)

            sp.wait_ge(scattered1, NB * K * DMA)
            sp.sem_inc(passed, 1)

            def load_nodes1(g, s, j):
                sp.wait_ge(g_turned, used(g - RING + 1))
                sp.sem_inc(passed, 1)
                sp.dma_start(node_in[:, s, 0:W], group(msum, g)).then_inc(s_in[s], DMA)
                sp.dma_start(node_in[:, s, W:], group(x1, g)).then_inc(x1_in[s], DMA)
            steps(sp, NG, load_nodes1)

        @block.gpsimd
        def _(pool):
            nc.gpsimd.memset(rows_i[:, 0], 0).then_inc(pads_set, 1)
            nc.gpsimd.iota(rows_i[:, 1], [[0, 2], [1, P]], base=PAD_TARGET, channel_multiplier=0).then_inc(pads_set, 1)
            nc.gpsimd.memset(rows_i[:, 2], 0).then_inc(pads_set, 1)
            nc.gpsimd.memset(rows_f[:, 3], 0.0).then_inc(pads_set, 1)
            nc.gpsimd.memset(ident[:, :], 0.0).then_inc(pool_set, 1)
            nc.gpsimd.memset(before[:, :], 1.0).then_inc(pool_set, 1)
            pool.wait_ge(pool_set, 2)
            nc.gpsimd.affine_select(out=ident[:, :], in_=ident[:, :], compare_op=ALU.not_equal, fill=1.0, base=0,
                                    pattern=[[-1, P]], channel_multiplier=1).then_inc(pool_set, 1)
            nc.gpsimd.affine_select(out=before[:, W - P:], in_=before[:, W - P:], compare_op=ALU.is_gt, fill=0.0,
                                    base=0, pattern=[[-1, P]], channel_multiplier=1).then_inc(pool_set, 1)
            nc.gpsimd.iota(spill_row[:, :, :], [[0, NB], [P, K]], base=N, channel_multiplier=1).then_inc(pool_set, 1)
            nc.gpsimd.memset(minus_half[:, :], -0.5).then_inc(pool_set, 1)
            nc.gpsimd.iota(type_no[:, :], [[1, T_TYPES]], base=0, channel_multiplier=0,
                           allow_small_or_imprecise_dtypes=True).then_inc(pool_set, 1)

            def scatter(i, indices, values, table, ready, done):
                pool.wait_ge(ready, i + 1)
                pool.sem_inc(passed, 1)
                pool.wait_ge(done, used(i * K * DMA))
                pool.sem_inc(passed, 1)
                for k in range(K):
                    nc.gpsimd.indirect_dma_start(
                        table, bass.IndirectOffsetOnAxis(ap=indices[:, k:k + 1], axis=0),
                        values[:, k * P:(k + 1) * P], None, compute_op=ALU.add).then_inc(done, DMA)

            def gather(i, s, table, width, made, done):
                pool.wait_ge(made, i + 1)
                pool.sem_inc(passed, 1)
                for k in range(width):
                    nc.gpsimd.indirect_dma_start(
                        xg[:, s, k, :], None, table,
                        bass.IndirectOffsetOnAxis(ap=gidx_slot[:, s, k:k + 1], axis=0)).then_inc(done[s], DMA)

            pool.wait_ge(index_ready, 1)
            pool.sem_inc(passed, 1)
            LEAD = 10
            for i in range(LEAD):
                gather(i, i % RING, x, 2 * K, gidx_made, gathered)
            pool.wait_ge(spill_zeroed, DMA)
            for c in range(2):
                pool.wait_ge(agg_set[c], CCHUNKS // 2 * DMA)

            def edge_step(i, s, _):
                scatter(i, sidx_slot[:, s, :], total0[:, s, :], agg, total_ready, scattered)
                if in_range(i + LEAD, NB):
                    gather(i + LEAD, (s + LEAD) % RING, x, 2 * K, gidx_made, gathered)
            for i in range(DEEP):
                edge_step(i, i, 0)
            turns = (NB - LEAD) // DEEP
            with pool.Fori(1, turns) as j:
                for s in range(DEEP):
                    edge_step(j * DEEP + s, s, j)
            for i in range(turns * DEEP, NB):
                edge_step(i, i % DEEP, turns)

            pool.wait_ge(msum_zeroed, ZCHUNKS * DMA)
            pool.sem_inc(passed, 1)
            for s in range(RING):
                pool.wait_ge(x1_out[s], ((NG0 - 1 - s) // RING + 1) * DMA)
                pool.sem_inc(passed, 1)
            for i in range(RING):
                gather(i, i, x1, K, gidx1_made, gathered1)

            def edge_step1(i, s, _):
                scatter(i, sidx_slot[:, s, :], total[:, s, :], msum, msg_ready, scattered1)
                if in_range(i + RING, NB):
                    gather(i + RING, s, x1, K, gidx1_made, gathered1)
            for i in range(RING):
                edge_step1(i, i, 0)
            turns = (NB - RING) // RING
            with pool.Fori(1, turns) as j:
                for s in range(RING):
                    edge_step1(j * RING + s, s, j)
            for i in range(turns * RING, NB):
                edge_step1(i, i % RING, turns)

            def inverse_std(c, added, value, ready):
                nc.gpsimd.tensor_scalar(n_var[:, c, 0:K], n_mv[:, c, 0:K, 1], EPS, None, ALU.add).then_inc(added, 1)
                pool.wait_ge(added, value)
                pool.sem_inc(passed, 1)
                nc.gpsimd.tensor_tensor(n_rstd[:, c, 0:K], n_var[:, c, 0:K], minus_half[:, :], ALU.pow).then_inc(ready, 1)

            def gru_step(g, s, j):
                c = s % 2
                if in_range(g - 3, NG):
                    pool.wait_ge(ymv_ready, g - 2)
                    pool.sem_inc(passed, 1)
                    inverse_std(1 - c, yeps_done, g - 2, yrstd_ready)
                if in_range(g - 2, NG):
                    pool.wait_ge(zx_ready, g - 1)
                    pool.sem_inc(passed, 1)
                    pool.wait_ge(back_done, used(g - 3))
                    pool.sem_inc(passed, 1)
                    nc.gpsimd.tensor_tensor(yt_sb[:, c, :], zx_sb[:, c, :], zn_sb[:, c, :], ALU.subtract)\
                        .then_inc(yt_ready, 1)
                if in_range(g, NG):
                    pool.wait_ge(xt1_ready, g + 1)
                    pool.sem_inc(passed, 1)
                    nc.gpsimd.tensor_tensor(xt1_parts[:, c, 1, :], xt1[:, s, :], as_f32(xt1_parts[:, c, 0, :]),
                                            ALU.subtract).then_inc(xtl_ready, 1)
            steps(pool, NG, gru_step, lag=3)

        @block.tensor
        def _(pe):
            def mm(to, left, right, start=True, stop=True):
                return nc.tensor.matmul(to, left, right, start=start, stop=stop)

            pe.wait_ge(pool_set, 3)
            pe.wait_ge(rows_ready, 1)
            for n in range(4):
                for c in range(2):
                    at = (n // 2) * W + (n % 2) * TILES + c * HALF
                    last = nc.tensor.transpose(turned_ps[:, at:at + HALF], rows_f[0:HALF, n, c, :],
                                               ident[0:HALF, 0:HALF])
            last.then_inc(setup_turned, 1)
            pe.wait_ge(weights_in, WEIGHT_LOADS * DMA)
            nc.tensor.transpose(bank[2][:, 0:P], wmsg_raw[:, :], ident[:, :])
            for b in range(3):
                nc.tensor.transpose(bank[0][:, b * P:(b + 1) * P], wih_raw[:, b, :], ident[:, :])
            for b in range(3):
                last = nc.tensor.transpose(bank[1][:, b * P:(b + 1) * P], whh_raw[:, b, :], ident[:, :])
            last.then_inc(setup_turned, 1)
            pe.wait_ge(weights_ready, 1)
            pe.wait_ge(index_ready, 1)

            def turn(ps, rows):
                for k in range(K):
                    last = nc.tensor.transpose(ps[:, k * P:(k + 1) * P], rows[:, k * P:(k + 1) * P], ident[:, :])
                return last

            def equal_sums(ps, values, equal):
                for k in reversed(range(K)):
                    n = (k + 1) * P
                    last = mm(ps[:, 0:n], values(k), equal[:, eq_at(k):eq_at(k) + n],
                              start=(k == K - 1), stop=(k == 0))
                return last

            h1t_ps, h1_ps, h1n_ps, h2t_ps, h2_ps, sumt_ps = bank
            sum_ps = h1t_ps

            def edge_step(i, s, j):
                c = s % 2
                if in_range(i, NB):
                    pe.wait_ge(gathered[s], (j + 1) * 2 * K * DMA)
                    pe.wait_ge(xt_ready, used(i))
                    for k in range(2 * K):
                        last = nc.tensor.transpose(turned_ps[:, k * P:(k + 1) * P], xg[:, s, k, :], ident[:, :])
                    last.then_inc(xg_turned, 1)
                if in_range(i - 1, NB):
                    pe.wait_ge(h1n_ready, used(i))
                    pe.wait_ge(y1_ready, used(i - 1))
                    turn(h1n_ps, h1n[:, 1 - c]).then_inc(h1n_turned, 1)
                if in_range(i, NB):
                    pe.wait_ge(xt_ready, i + 1)
                    pe.wait_ge(total_ready, used(i - 3))
                    mm(h1t_ps[:, :], w1_sb[:, 0, :], xt[:, c, 0:W], stop=False)
                    mm(h1t_ps[:, :], w1_sb[:, 1, :], xt[:, c, W:], start=False).then_inc(h1_done, 1)
                if in_range(i - 1, NB):
                    pe.wait_ge(act1_ready, i)
                    pe.wait_ge(h2t_ready, used(i - 1))
                    mm(h2t_ps[:, :], w2_sb[:, :], act1[:, 1 - c, :]).then_inc(h2_done, 1)
                if in_range(i, NB):
                    pe.wait_ge(h1t_ready, i + 1)
                    pe.wait_ge(h1n_ready, used(i))
                    turn(h1_ps, h1t_sb).then_inc(h1_back, 1)
                if in_range(i - 1, NB):
                    pe.wait_ge(h2t_ready, i)
                    pe.wait_ge(h2n_ready, used(i - 1))
                    turn(h2_ps, h2t_sb).then_inc(h2_back, 1)
                if in_range(i - 2, NB):
                    pe.wait_ge(hout_ready, i - 1)
                    pe.wait_ge(equal_made, i - 1)
                    pe.wait_ge(sumt_ready, used(i - 2))
                    equal_sums(sumt_ps, lambda k: hout[:, c, k * P:(k + 1) * P], equal[:, c]).then_inc(sums_done, 1)
                if in_range(i - 2, NB):
                    pe.wait_ge(sumt_ready, i - 1)
                    pe.wait_ge(h1t_ready, i + 1 if in_range(i, NB) else NB)
                    turn(sum_ps, sumt_sb).then_inc(sums_back, 1)
            steps(pe, NB, edge_step, lag=2)

            msgt_ps, msg_ps = bank[4], bank[5]

            def edge_step1(i, s, j):
                c = s % 2
                if in_range(i - 1, NB):
                    pe.wait_ge(at_ready, i)
                    pe.wait_ge(msgt_ready, used(i - 1))
                    mm(msgt_ps[:, :], wmsg_t[:, :], at_sb[:, 1 - c, :], stop=False)
                    mm(msgt_ps[:, :], embb[:, :], ct_sb[:, 1 - c, :], start=False).then_inc(msg_done, 1)
                if in_range(i, NB):
                    pe.wait_ge(gathered1[s], (j + 1) * K * DMA)
                    pe.wait_ge(equal1_made, i + 1)
                    pe.wait_ge(at_ready, used(i - 1))
                    equal_sums(bank[c], lambda k: xg[:, s, k, :], as_f32(equal1[:, c]))
                    equal_sums(bank[2 + c][0:T_TYPES], lambda k: onehot[:, c, k, :], equal1[:, c])\
                        .then_inc(edge_sums, 1)
                if in_range(i - 1, NB):
                    pe.wait_ge(msgt_ready, i)
                    pe.wait_ge(msg_ready, used(i - 1))
                    turn(msg_ps, msgt_sb).then_inc(msg_back, 1)
            steps(pe, NB, edge_step1, lag=1)

            r_ps, hn_ps, z_ps, in_ps = bank[0], bank[1], bank[2], bank[3]

            def product(ps, weights, gate, values, start=True, stop=True):
                cols = slice(gate * P, (gate + 1) * P)
                mm(ps[:, :], weights[:, 0, cols], values[:, 0, :], start=start, stop=False)
                mm(ps[:, :], weights[:, 1, cols], values[:, 0, :], start=False, stop=False)
                return mm(ps[:, :], weights[:, 0, cols], values[:, 1, :], start=False, stop=stop)

            def gru_step(g, s, j):
                c = s % 2
                if in_range(g, NG):
                    pe.wait_ge(s_in[s], (j + 1) * DMA)
                    pe.wait_ge(mt_ready, used(g))
                    for k in range(K):
                        nc.tensor.transpose(turned_ps[:, k * P:(k + 1) * P], node_in[:, s, k * P:(k + 1) * P],
                                            ident[:, :])
                    pe.wait_ge(x1_in[s], (j + 1) * DMA)
                    pe.wait_ge(xt1_ready, used(g))
                    for k in range(K):
                        last = nc.tensor.transpose(turned_ps[:, W + k * P:W + (k + 1) * P],
                                                   node_in[:, s, W + k * P:W + (k + 1) * P], ident[:, :])
                    last.then_inc(g_turned, 1)
                if in_range(g - 1, NG):
                    m, h = mt[:, 1 - c], xt1_parts[:, 1 - c]
                    pe.wait_ge(mt_ready, g)
                    pe.wait_ge(r_ready, used(g - 1))
                    product(r_ps, wih_t, 0, m, stop=False)
                    pe.wait_ge(xtl_ready, g)
                    product(r_ps, whh_t, 0, h, start=False).then_inc(r_done, 1)
                    pe.wait_ge(rh_ready, used(g - 1))
                    product(hn_ps, whh_t, 2, h).then_inc(hn_done, 1)
                    pe.wait_ge(pre_ready, used(g - 1))
                    product(in_ps, wih_t, 2, m).then_inc(in_done, 1)
                    pe.wait_ge(z_ready, used(g - 1))
                    product(z_ps, wih_t, 1, m, stop=False)
                    product(z_ps, whh_t, 1, h, start=False).then_inc(z_done, 1)
                if in_range(g - 2, NG):
                    back_ps = bank[4 + c]
                    pe.wait_ge(yt_ready, g - 1)
                    pe.wait_ge(o_ready, used(g - 3))
                    for k in range(K):
                        last = nc.tensor.transpose(back_ps[:, k * P:(k + 1) * P],
                                                   yt_sb[:, c, k * P:(k + 1) * P], ident[:, :])
                    last.then_inc(back_done, 1)
            steps(pe, NG, gru_step, lag=2)

        @block.scalar
        def _(act):
            h1t_ps, h1_ps, h1n_ps, h2t_ps, h2_ps, sumt_ps = bank
            sum_ps = h1t_ps
            act.wait_ge(cols_made, 1)
            act.wait_ge(weights_ready, 1)

            def normalise_rows(to, ps, scales, biases, ready):
                for k in range(K):
                    last = nc.scalar.activation(to[:, k * P:(k + 1) * P], ps[:, k * P:(k + 1) * P], ACT.Identity,
                                                bias=biases[:, k:k + 1], scale=scales[:, k:k + 1])
                last.then_inc(ready, 1)

            def edge_step(i, s, j):
                c = s % 2
                if in_range(i, NB):
                    act.wait_ge(xg_turned, i + 1)
                    act.wait_ge(h1_done, used(i - 1))
                    nc.scalar.activation(xt[:, c, 0:W], turned_ps[:, 0:W], ACT.Copy)
                    nc.scalar.activation(xt[:, c, W:], turned_ps[:, W:], ACT.Copy).then_inc(xt_ready, 1)
                    nc.scalar.activation(gidx_slot[:, s % RING, :], gather_idx[:, i + RING, :], ACT.Copy)\
                        .then_inc(gidx_made, 1)
                if in_range(i - 1, NB):
                    act.wait_ge(h1n_turned, i)
                    act.wait_ge(act1_ready, used(i - 2))
                    nc.scalar.activation(y1[:, 1 - c, :], h1n_ps[:, :], ACT.Identity, bias=be1_col[:, 0:1],
                                         scale=g1_col[:, 0:1]).then_inc(y1_ready, 1)
                if in_range(i - 2, NB):
                    act.wait_ge(shift2_ready, i - 1)
                    act.wait_ge(h2g_ready, used(i - 2))
                    normalise_rows(h2n, h2_ps, rstd[:, 1], shift[:, 1], h2n_ready)
                if in_range(i, NB):
                    act.wait_ge(h1_done, i + 1)
                    act.wait_ge(h1_back, used(i))
                    nc.scalar.activation(h1t_sb[:, :], h1t_ps[:, :], ACT.Identity, bias=b1_col[:, 0:1])\
                        .then_inc(h1t_ready, 1)
                if in_range(i - 1, NB):
                    act.wait_ge(h2_done, i)
                    act.wait_ge(h2_back, used(i - 1))
                    nc.scalar.activation(h2t_sb[:, :], h2t_ps[:, :], ACT.Identity, bias=b2_col[:, 0:1])\
                        .then_inc(h2t_ready, 1)
                if in_range(i, NB):
                    act.wait_ge(mv1_ready, i + 1)
                    nc.scalar.activation(std[:, 0, :], mv[:, 0, :, 1], ACT.Sqrt, bias=eps_col[:, 0:1])\
                        .then_inc(std1_ready, 1)
                if in_range(i, NB):
                    act.wait_ge(shift1_ready, i + 1)
                    act.wait_ge(h1n_turned, used(i - 1))
                    normalise_rows(h1n[:, c], h1_ps, rstd[:, 0], shift[:, 0], h1n_ready)
                if in_range(i - 1, NB):
                    act.wait_ge(mv2_ready, i)
                    nc.scalar.activation(std[:, 1, :], mv[:, 1, :, 1], ACT.Sqrt, bias=eps_col[:, 0:1])\
                        .then_inc(std2_ready, 1)
                if in_range(i - 2, NB):
                    act.wait_ge(sums_done, i - 1)
                    act.wait_ge(sums_back, used(i - 2))
                    nc.scalar.activation(sumt_sb[:, :], sumt_ps[:, :], ACT.Copy).then_inc(sumt_ready, 1)
                if in_range(i - 2, NB):
                    act.wait_ge(sums_back, i - 1)
                    act.wait_ge(scattered, used((i - DEEP + 1) * K * DMA))
                    act.wait_ge(sidx_made, i - 1)
                    nc.scalar.activation(sidx_slot[:, (s - 2) % DEEP, :], scatter_idx[:, i - 2, :], ACT.Copy)
                    nc.scalar.activation(total0[:, (s - 2) % DEEP, :], sum_ps[:, :], ACT.Copy)\
                        .then_inc(total_ready, 1)
            steps(act, NB, edge_step, lag=2, body=DEEP)

            def node_step(g, s, j):
                c = s % 2
                if in_range(g, NG0):
                    act.wait_ge(nmv_ready, g + 1)
                    nc.scalar.activation(n_var[:, c, :], n_mv[:, c, :, 1], ACT.Sqrt, bias=eps_col[:, 0:1])\
                        .then_inc(nstd_ready, 1)
                if in_range(g - 1, NG0):
                    act.wait_ge(nshift_ready, g)
                    if not isinstance(g, int) or g > RING:
                        act.wait_ge(x1_out[(s - 1) % RING], (2 * j + (s - 1) // RING) * DMA)
                    for k in range(DVE_TILES, 2 * K):
                        last = nc.scalar.activation(
                            result_of(s - 1)[:, k * P:(k + 1) * P], sums_of(s - 1)[:, k * P:(k + 1) * P],
                            ACT.Identity, bias=n_shift[:, 1 - c, k:k + 1], scale=n_rstd[:, 1 - c, k:k + 1])
                    last.then_inc(x1_ready, 1)
            steps(act, NG0, node_step, lag=1, body=DEEP)

            msgt_ps, msg_ps = bank[4], bank[5]
            nc.scalar.activation(gidx_slot[:, :, :], gather_idx[:, 0:RING, :], ACT.Copy).then_inc(gidx1_made, RING)

            def edge_step1(i, s, j):
                c = s % 2
                if in_range(i - 1, NB):
                    act.wait_ge(msg_done, i)
                    act.wait_ge(msg_back, used(i - 1))
                    nc.scalar.activation(msgt_sb[:, :], msgt_ps[:, :], ACT.Copy).then_inc(msgt_ready, 1)
                if in_range(i, NB):
                    act.wait_ge(edge_sums, i + 1)
                    act.wait_ge(msg_done, used(i - 1))
                    nc.scalar.activation(at_sb[:, c, :], bank[c][:, :], ACT.Copy)
                    nc.scalar.activation(ct_sb[:, c, :], bank[2 + c][0:T_TYPES, :], ACT.Copy).then_inc(at_ready, 1)
                    nc.scalar.activation(gidx_slot[:, s, :], gather_idx[:, i + RING, :], ACT.Copy)\
                        .then_inc(gidx1_made, 1)
                if in_range(i - 1, NB):
                    act.wait_ge(msg_back, i)
                    act.wait_ge(scattered1, used((i - 3) * K * DMA))
                    nc.scalar.activation(sidx_slot[:, (s - 1) % RING, :], scatter_idx[:, i - 1, :], ACT.Copy)
                    nc.scalar.activation(total[:, (s - 1) % RING, :], msg_ps[:, :], ACT.Copy)\
                        .then_inc(msg_ready, 1)
            steps(act, NB, edge_step1, lag=1)

            r_ps, z_ps = bank[0], bank[2]

            def gru_step(g, s, j):
                c, b = s % 2, (s - 3) % RING
                if in_range(g - 2, NG):
                    act.wait_ge(z_done, g - 1)
                    act.wait_ge(zx_ready, used(g - 3))
                    nc.scalar.activation(z_sb[:, c, :], z_ps[:, :], ACT.Sigmoid, bias=brz_col[:, 1:2])\
                        .then_inc(z_ready, 1)
                if in_range(g, NG):
                    act.wait_ge(g_turned, g + 1)
                    act.wait_ge(z_done, used(g - 1))
                    nc.scalar.activation(mt[:, c, 0, :], turned_ps[:, 0:W], ACT.Copy).then_inc(mth_ready, 1)
                    nc.scalar.activation(xt1_parts[:, c, 0, :], turned_ps[:, W:], ACT.Copy)
                    act.wait_ge(zx_ready, used(g - RING + 1))
                    nc.scalar.activation(xt1[:, s, :], turned_ps[:, W:], ACT.Copy).then_inc(xt1_ready, 1)
                if in_range(g - 1, NG):
                    act.wait_ge(r_done, g)
                    act.wait_ge(rh_ready, used(g - 2))
                    nc.scalar.activation(r_sb[:, 1 - c, :], r_ps[:, :], ACT.Sigmoid, bias=brz_col[:, 0:1])\
                        .then_inc(r_ready, 1)
                if in_range(g - 3, NG):
                    act.wait_ge(yshift_ready, g - 2)
                    if not isinstance(g, int) or g - 3 >= RING:
                        act.wait_ge(out_done[b], (j if s >= 3 else j - 1) * DMA)
                    for k in range(K):
                        last = nc.scalar.activation(
                            ng_o[:, b, k * P:(k + 1) * P], bank[5 - c][:, k * P:(k + 1) * P], ACT.Identity,
                            bias=n_shift[:, 1 - c, k:k + 1], scale=n_rstd[:, 1 - c, k:k + 1])
                    last.then_inc(o_ready, 1)
                if in_range(g - 1, NG):
                    act.wait_ge(pre_ready, g)
                    act.wait_ge(zn_ready, used(g - 2))
                    nc.scalar.activation(n_sb[:, 1 - c, :], pre_n[:, 1 - c, :], ACT.Tanh, bias=bih_col[:, 2:3])\
                        .then_inc(n_ready, 1)
                if in_range(g - 3, NG):
                    act.wait_ge(o_ready, g - 2)
                    if isinstance(g, int) and g - 3 == NG - 1:
                        act.wait_ge(out_done[(s - 4) % RING], ((g - 4) // RING + 1) * DMA)
                    act.dma_start(group(out, g - 3), ng_o[:, b, :]).then_inc(out_done[b], DMA)
            steps(act, NG, gru_step, lag=3)
            for s in range(RING):
                act.wait_ge(out_done[s], ((NG - 1 - s) // RING + 1) * DMA)

        @block.vector
        def _(dve):
            nc.vector.memset(zeros[:, :], 0.0)
            nc.vector.memset(eps_col[:, :], EPS).then_inc(cols_made, 1)
            dve.wait_ge(edges_in, EDGE_LOADS * DMA)
            nc.vector.tensor_copy(rows_f[0:HALF, 0:3], rows_i[0:HALF]).then_inc(rows_ready, 1)
            dve.wait_ge(setup_turned, 1)
            dve.wait_ge(pool_set, 7)

            def turned(n):
                at = (n // 2) * W + (n % 2) * TILES
                return turned_ps[:, at:at + TILES].rearrange("p (b k) -> p b k", k=K)

            nc.vector.tensor_copy(gather_idx[:, 0:NB, 0:K], turned(0))
            nc.vector.tensor_scalar(gather_idx[:, 0:NB, K:], turned(1), float(N - 1), None, ALU.min)
            nc.vector.tensor_copy(dst_col[:, :, :], turned(1)).then_inc(cols_made, 1)
            nc.vector.tensor_scalar(type_col[:, :, :], turned(2), 0.0, float(T_TYPES - 1), ALU.max, ALU.min)
            nc.vector.tensor_copy(w_col[:, :, :], turned(3))
            nc.vector.memset(gather_idx[:, NB:, :], 0)
            dve.wait_ge(cols_made, 2)
            nc.vector.tensor_copy(gidx_slot[:, :, :], gather_idx[:, 0:RING, :]).then_inc(gidx_made, RING)
            nc.vector.tensor_tensor(to_spill[:, :, :], spill_row[:, :, :], dst_col[:, :, :], ALU.subtract)\
                .then_inc(index_ready, 1)
            dve.wait_ge(setup_turned, 2)
            nc.vector.tensor_copy(wmsg_t[:, :], bank[2][:, 0:P])
            nc.vector.tensor_copy(wih_t[:, 0, :], bank[0][:, 0:3 * P])
            nc.vector.tensor_copy(whh_t[:, 0, :], bank[1][:, 0:3 * P]).then_inc(high_made, 1)
            dve.wait_ge(high_made, 1)
            nc.vector.tensor_tensor(wih_t[:, 1, :], bank[0][:, 0:3 * P], as_f32(wih_t[:, 0, :]), ALU.subtract)
            nc.vector.tensor_tensor(whh_t[:, 1, :], bank[1][:, 0:3 * P], as_f32(whh_t[:, 0, :]), ALU.subtract)
            nc.vector.tensor_tensor(brz_col[:, :], bih_col[:, 0:2], bhh_col[:, 0:2], ALU.add)
            nc.vector.tensor_tensor(embb[:, :], emb_sb[:, :], bmsg_all[:, :], ALU.add).then_inc(weights_ready, 1)
            dve.wait_ge(index_ready, 1)

            h1_ps, h2_ps = bank[1], bank[4]

            def equalities(i, c, equal, weighted, made):
                for k in range(K):
                    n = (k + 1) * P
                    last = nc.vector.tensor_scalar(
                        equal[:, c, eq_at(k):eq_at(k) + n], dst_row[:, c, 0:n], dst_col[:, i, k:k + 1],
                        w_col[:, i, k:k + 1] if weighted else None, ALU.is_equal,
                        ALU.mult if weighted else ALU.bypass)
                last.then_inc(made, 1)

            def row_stats(ps, to_stats, to_mv, done, value, ready, tiles=K):
                for k in range(tiles):
                    last = nc.vector.bn_stats(to_stats[:, k, :], ps[:, k * P:(k + 1) * P])
                last.then_inc(done, 1)
                dve.wait_ge(done, value)
                dve.sem_inc(passed, 1)
                for k in range(tiles):
                    last = nc.vector.bn_aggr(to_mv[:, k, :], to_stats[:, k, :])
                last.then_inc(ready, 1)

            def every_tile(row):
                return row[:, None, :].to_broadcast([P, K, P])

            def tiles(a):
                return a.rearrange("p (k f) -> p k f", k=K)

            def scales(n, c, got_std, value, recip, ready):
                dve.wait_ge(got_std, value)
                nc.vector.reciprocal(rstd[:, n, :], std[:, n, :]).then_inc(recip, 1)
                dve.wait_ge(recip, value)
                nc.vector.scalar_tensor_tensor(out=shift[:, n, :], in0=mv[:, n, :, 0], scalar=-1.0,
                                               in1=rstd[:, n, :], op0=ALU.mult, op1=ALU.mult).then_inc(ready, 1)

            def edge_step(i, s, j):
                c = s % 2
                b, e = i - 1, 1 - c
                if in_range(i - 1, NB):
                    dve.wait_ge(y1_ready, i)
                    dve.wait_ge(h2_done, used(i - 2))
                    nc.vector.scalar_tensor_tensor(out=act1[:, 1 - c, :], in0=y1[:, 1 - c, :], scalar=SLOPE,
                                                   in1=y1[:, 1 - c, :], op0=ALU.mult, op1=ALU.max)\
                        .then_inc(act1_ready, 1)
                if in_range(i - 2, NB):
                    dve.wait_ge(h2n_ready, i - 1)
                    nc.vector.tensor_tensor(tiles(h2g[:, :]), tiles(h2n[:, :]), every_tile(g2_all), ALU.mult)\
                        .then_inc(h2g_ready, 1)
                    dve.wait_ge(h2g_ready, i - 1)
                    nc.vector.tensor_tensor(tiles(h2b[:, :]), tiles(h2g[:, :]), every_tile(be2_all), ALU.add)\
                        .then_inc(h2b_ready, 1)
                    dve.wait_ge(h2b_ready, i - 1)
                    dve.wait_ge(sums_done, used(i - 3))
                    nc.vector.scalar_tensor_tensor(out=hout[:, c, :], in0=h2b[:, :], scalar=SLOPE,
                                                   in1=h2b[:, :], op0=ALU.mult, op1=ALU.max)\
                        .then_inc(hout_ready, 1)
                if in_range(i, NB):
                    dve.wait_ge(h1_back, i + 1)
                    dve.wait_ge(h1n_ready, used(i))
                    row_stats(h1_ps, stats[:, 0], mv[:, 0], st1_done, i + 1, mv1_ready)
                if in_range(i, NB):
                    scales(0, c, std1_ready, i + 1, rstd1_ready, shift1_ready)
                if in_range(i - 1, NB):
                    dve.wait_ge(h2_back, i)
                    row_stats(h2_ps, stats[:, 1], mv[:, 1], st2_done, i, mv2_ready)
                if in_range(i - 1, NB):
                    dve.wait_ge(dstrow_in[e], (2 * j + (s - 1) // 2 + 1) * DMA)
                    for k in range(K):
                        n = (k + 1) * P
                        last = nc.vector.scalar_tensor_tensor(
                            out=junk[:, k, 0:n], in0=dst_row[:, e, 0:n], scalar=dst_col[:, b, k:k + 1],
                            in1=before[:, W - n:], op0=ALU.is_equal, op1=ALU.mult, accum_out=dups[:, e, k:k + 1])
                    last.then_inc(dup_done, 1)
                    scales(1, e, std2_ready, i, rstd2_ready, shift2_ready)
                if in_range(i - 1, NB):
                    dve.wait_ge(dup_done, i)
                    nc.vector.scalar_tensor_tensor(out=moved[:, e, :], in0=dups[:, e, :], scalar=0.0,
                                                   in1=to_spill[:, b, :], op0=ALU.is_gt, op1=ALU.mult)\
                        .then_inc(moved_done, 1)
                    dve.wait_ge(sums_done, used(i - 2))
                    equalities(b, e, equal, True, equal_made)
                    dve.wait_ge(moved_done, i)
                    nc.vector.tensor_tensor(scatter_idx[:, b, :], moved[:, e, :], dst_col[:, b, :], ALU.add)\
                        .then_inc(sidx_made, 1)
            steps(dve, NB, edge_step, lag=2)

            def node_step(g, s, j):
                c = s % 2
                if in_range(g, NG0):
                    dve.wait_ge(agg_in[s], (j + 1) * DMA)
                    dve.sem_inc(passed, 1)
                    row_stats(sums_of(s), n_stats[:, c], n_mv[:, c], nst_done, g + 1, nmv_ready, 2 * K)
                if in_range(g - 1, NG0):
                    dve.wait_ge(nstd_ready, g)
                    dve.wait_ge(x1_ready, used(g - 2))
                    nc.vector.reciprocal(n_rstd[:, 1 - c, :], n_var[:, 1 - c, :]).then_inc(nrstd_ready, 1)
                    dve.wait_ge(nrstd_ready, g)
                    nc.vector.scalar_tensor_tensor(out=n_shift[:, 1 - c, :], in0=n_mv[:, 1 - c, :, 0], scalar=-1.0,
                                                   in1=n_rstd[:, 1 - c, :], op0=ALU.mult, op1=ALU.mult)\
                        .then_inc(nshift_ready, 1)
                    if not isinstance(g, int) or g > RING:
                        dve.wait_ge(x1_out[(s - 1) % RING], (2 * j + (s - 1) // RING) * DMA)
                    for k in range(DVE_TILES):
                        last = nc.vector.tensor_scalar(
                            result_of(s - 1)[:, k * P:(k + 1) * P], sums_of(s - 1)[:, k * P:(k + 1) * P],
                            n_mv[:, 1 - c, k, 0:1], n_rstd[:, 1 - c, k:k + 1], ALU.subtract, ALU.mult)
                    last.then_inc(x1_first, 1)
            steps(dve, NG0, node_step, lag=1, body=DEEP)

            def edge_step1(i, s, j):
                c = s % 2
                dve.wait_ge(dstrow1_in[c], (2 * j + s // 2 + 1) * DMA)
                dve.wait_ge(edge_sums, used(i - 1))
                nc.vector.tensor_tensor(
                    onehot[:, c], type_col[:, i, :].rearrange("p (k a) -> p k a", a=1).to_broadcast([P, K, T_TYPES]),
                    type_no[:, None, :].to_broadcast([P, K, T_TYPES]), ALU.is_equal)
                equalities(i, c, equal1, False, equal1_made)
            steps(dve, NB, edge_step1)

            hn_ps, in_ps = bank[1], bank[3]

            def gru_step(g, s, j):
                c = s % 2
                if in_range(g - 3, NG):
                    dve.wait_ge(back_done, g - 2)
                    row_stats(bank[5 - c], n_stats[:, 1 - c], n_mv[:, 1 - c], yst_done, g - 2, ymv_ready)
                if in_range(g - 2, NG):
                    dve.wait_ge(n_ready, g - 1)
                    dve.wait_ge(z_ready, g - 1)
                    dve.wait_ge(yt_ready, used(g - 3))
                    nc.vector.scalar_tensor_tensor(out=zn_sb[:, c, :], in0=z_sb[:, c, :], scalar=-1.0,
                                                   in1=n_sb[:, c, :], op0=ALU.add, op1=ALU.mult)\
                        .then_inc(zn_ready, 1)
                    nc.vector.scalar_tensor_tensor(out=zx_sb[:, c, :], in0=z_sb[:, c, :], scalar=1.0,
                                                   in1=xt1[:, (s - 2) % RING, :], op0=ALU.add, op1=ALU.mult)\
                        .then_inc(zx_ready, 1)
                if in_range(g, NG):
                    dve.wait_ge(mth_ready, g + 1)
                    nc.vector.tensor_tensor(mt[:, c, 1, :], turned_ps[:, 0:W], as_f32(mt[:, c, 0, :]), ALU.subtract)\
                        .then_inc(mt_ready, 1)
                if in_range(g - 3, NG):
                    dve.wait_ge(yrstd_ready, g - 2)
                    nc.vector.scalar_tensor_tensor(out=n_shift[:, 1 - c, 0:K], in0=n_mv[:, 1 - c, 0:K, 0], scalar=-1.0,
                                                   in1=n_rstd[:, 1 - c, 0:K], op0=ALU.mult, op1=ALU.mult)\
                        .then_inc(yshift_ready, 1)
                if in_range(g - 1, NG):
                    dve.wait_ge(hn_done, g)
                    dve.wait_ge(r_ready, g)
                    dve.wait_ge(pre_ready, used(g - 2))
                    nc.vector.scalar_tensor_tensor(out=rh_sb[:, 1 - c, :], in0=hn_ps[:, :], scalar=bhh_col[:, 2:3],
                                                   in1=r_sb[:, 1 - c, :], op0=ALU.add, op1=ALU.mult)\
                        .then_inc(rh_ready, 1)
                    dve.wait_ge(rh_ready, g)
                    dve.wait_ge(in_done, g)
                    dve.wait_ge(n_ready, used(g - 2))
                    nc.vector.tensor_tensor(pre_n[:, 1 - c, :], rh_sb[:, 1 - c, :], in_ps[:, :], ALU.add)\
                        .then_inc(pre_ready, 1)
            steps(dve, NG, gru_step, lag=3)


EDGE_LOADS = 12
DVE_TILES = 1
WEIGHT_LOADS = 15

_INS = ['x', 'src', 'dst', 'edge_type_9', 'edge_weight', 'L0_gnn_w1', 'L0_gnn_b1', 'L0_gnn_g1', 'L0_gnn_be1',
        'L0_gnn_w2', 'L0_gnn_b2', 'L0_gnn_g2', 'L0_gnn_be2', 'L1_gnn_W_msg', 'L1_gnn_b_msg', 'L1_gnn_edge_embed',
        'L1_gnn_W_ih', 'L1_gnn_W_hh', 'L1_gnn_b_ih', 'L1_gnn_b_hh']


def kernel(**inputs):
    import numpy as _np
    import concourse.bacc as _bacc
    from concourse import mybir as _mybir
    from concourse.bass_utils import run_bass_kernel_spmd as _run

    nc = _bacc.Bacc("TRN2", target_bir_lowering=False, num_devices=1)
    arrays, args = {}, []
    for name in _INS:
        a = _np.ascontiguousarray(inputs[name])
        arrays[f"in_{name}"] = a
        args.append(nc.dram_tensor(f"in_{name}", a.shape, _mybir.dt.from_np(a.dtype), kind="ExternalInput").ap())
    shape = inputs['x'].shape
    args.append(nc.dram_tensor("out_0", shape, _mybir.dt.float32, kind="ExternalOutput").ap())
    gnn_kernel(nc, *args)
    r = _run(nc, [arrays], core_ids=[0])
    return r.results[0]["out_0"]
```
